# Optimizing a Trainium2 kernel written in Bass

```python
import numpy as np
import jax
import jax.numpy as jnp

def _softmax(x, axis=-1):
    return jax.nn.softmax(x, axis=axis)

def _gelu(x):
    return jax.nn.gelu(x, approximate=True)

def _silu(x):
    return jax.nn.silu(x)

def _sigmoid(x):
    return jax.nn.sigmoid(x)

def _layernorm(x, axis=-1, eps=1e-05):
    m = jnp.mean(x, axis=axis, keepdims=True)
    v = jnp.var(x, axis=axis, keepdims=True)
    return (x - m) / jnp.sqrt(v + eps)

def _scatter_add(tgt, idx, src, axis=0):
    return tgt.at[idx].add(src)

def _segment_sum(src, seg, n):
    return jax.ops.segment_sum(src, seg, n)
kernel_name = 'mk_decoder_postln_d2_seqx_r4_93d3ae'

def setup_inputs(seed: int=0):
    np.random.seed(seed)
    _w = jnp.asarray

    def _rec_inputs():
        import jax
        import jax.numpy as jnp
        _rk = jax.random.key(seed)
        x = 0.0003765 + 1 * jax.random.normal(jax.random.fold_in(_rk, 1), (4, 512, 256), jnp.float32)
        _lenS = 512 - jax.random.randint(jax.random.fold_in(_rk, 7), (4,), 0, max(1, 512 // 4) + 1, jnp.int32)
        _lenS2 = 512 - jax.random.randint(jax.random.fold_in(_rk, 8), (4,), 0, max(1, 512 // 4) + 1, jnp.int32)
        _ctx_1024P = jax.random.normal(jax.random.fold_in(_rk, 11), (4, 16, 256), jnp.float32)
        _ctx_1024c = jax.random.dirichlet(jax.random.fold_in(_rk, 511), 0.3 * jnp.ones((16,), jnp.float32), (4, 512))
        _ctx_1024t = jnp.einsum('bsk,bkd->bsd', _ctx_1024c, _ctx_1024P)
        _ctx_1024t = _ctx_1024t * jax.lax.rsqrt(jnp.mean(jnp.square(_ctx_1024t)) + 1e-12) * 0.953939
        ctx_1024 = -0.000292821 + 1.00034 * (_ctx_1024t + 0.3 * jax.random.normal(jax.random.fold_in(_rk, 611), (4, 512, 256), jnp.float32))
        _validS = jnp.arange(512)[None, :] < _lenS[:, None]
        _validS2 = jnp.arange(512)[None, :] < _lenS2[:, None]
        _causal = jnp.tril(jnp.ones((512, 512), dtype=bool))
        mask_BxSxS2_bk1 = jnp.broadcast_to(_validS2[:, None, :], (4, 512, 512))
        return (x, ctx_1024, mask_BxSxS2_bk1)
    x, ctx_1024, mask_BxSxS2_bk1 = _rec_inputs()

    def _L0_attn_setup():
        import jax, jax.numpy as jnp
        import numpy as np
        from jax import lax
        B_, L_, D_MODEL = (2, 256, 256)
        D_STATE, D_CONV, EXPAND = (16, 4, 2)
        D_INNER = EXPAND * D_MODEL
        DT_RANK = (D_MODEL + 15) // 16
        LN_EPS = 1e-05

        def _silu(v):
            return v * jax.nn.sigmoid(v)

        def _mamba_params(key):
            ks = jax.random.split(key, 6)
            g = lambda k, shp, sc: jax.random.normal(k, shp, jnp.float32) * sc
            return {'in_proj_w': g(ks[0], (2 * D_INNER, D_MODEL), D_MODEL ** (-0.5)), 'conv_w': g(ks[1], (D_INNER, D_CONV), D_CONV ** (-0.5)), 'conv_b': jnp.zeros((D_INNER,), jnp.float32), 'x_proj_w': g(ks[2], (DT_RANK + 2 * D_STATE, D_INNER), D_INNER ** (-0.5)), 'dt_proj_w': g(ks[3], (D_INNER, DT_RANK), DT_RANK ** (-0.5)), 'dt_proj_b': jax.random.uniform(ks[4], (D_INNER,), jnp.float32, -4.0, -2.0), 'A_log': jnp.log(jnp.broadcast_to(jnp.arange(1, D_STATE + 1, dtype=jnp.float32), (D_INNER, D_STATE))), 'D': jnp.ones((D_INNER,), jnp.float32), 'out_proj_w': g(ks[5], (D_MODEL, D_INNER), D_INNER ** (-0.5))}

        def _mamba(x, in_proj_w, conv_w, conv_b, x_proj_w, dt_proj_w, dt_proj_b, A_log, D, out_proj_w):
            b, l, _ = x.shape
            xz = x @ in_proj_w.T
            xi, z = jnp.split(xz, 2, axis=-1)
            xp = jnp.pad(xi, ((0, 0), (D_CONV - 1, 0), (0, 0)))
            xc = conv_b + sum((xp[:, k:k + l, :] * conv_w[:, k] for k in range(D_CONV)))
            xc = _silu(xc)
            dbl = xc @ x_proj_w.T
            dt = jax.nn.softplus(dbl[..., :DT_RANK] @ dt_proj_w.T + dt_proj_b)
            Bm = dbl[..., DT_RANK:DT_RANK + D_STATE]
            Cm = dbl[..., DT_RANK + D_STATE:]
            A = -jnp.exp(A_log)
            dA = jnp.exp(dt[..., None] * A)
            dBu = (dt * xc)[..., None] * Bm[:, :, None, :]

            def step(h, inp):
                dA_t, dBu_t, C_t = inp
                h = dA_t * h + dBu_t
                return (h, jnp.einsum('bdn,bn->bd', h, C_t))
            h0 = jnp.zeros((b, D_INNER, D_STATE), x.dtype)
            _, ys = lax.scan(step, h0, (dA.transpose(1, 0, 2, 3), dBu.transpose(1, 0, 2, 3), Cm.transpose(1, 0, 2)))
            y = ys.transpose(1, 0, 2) + xc * D
            y = y * _silu(z)
            return y @ out_proj_w.T
        key = jax.random.key(seed)
        kx, kf, kb = jax.random.split(key, 3)
        inp = {'x': jax.random.normal(kx, (B_, L_, D_MODEL), jnp.float32)}
        for pref, k in (('fwd_', kf), ('bwd_', kb)):
            for name, val in _mamba_params(k).items():
                inp[pref + name] = val
        inp['ln_gamma'] = jnp.ones((D_MODEL,), jnp.float32)
        inp['ln_beta'] = jnp.zeros((D_MODEL,), jnp.float32)
        return inp
    _L0_attn_all = _L0_attn_setup()
    _L0_attn_in = {k: v for k, v in _L0_attn_all.items() if k in ('fwd_in_proj_w', 'fwd_conv_w', 'fwd_conv_b', 'fwd_x_proj_w', 'fwd_dt_proj_w', 'fwd_dt_proj_b', 'fwd_A_log', 'fwd_D', 'fwd_out_proj_w', 'bwd_in_proj_w', 'bwd_conv_w', 'bwd_conv_b', 'bwd_x_proj_w', 'bwd_dt_proj_w', 'bwd_dt_proj_b', 'bwd_A_log', 'bwd_D', 'bwd_out_proj_w', 'ln_gamma', 'ln_beta')}
    del _L0_attn_all

    def _L0_xattn_setup():
        import jax, jax.numpy as jnp
        import numpy as np
        N_HEAD, D_MODEL, DQ, DK, DV = (16, 256, 64, 64, 64)
        B, LQ, LK = (2, 512, 512)
        EPS = 0.001

        def _layer_norm(x, gamma, beta):
            mean = jnp.mean(x, axis=-1, keepdims=True)
            std = jnp.std(x, axis=-1, keepdims=True, ddof=1)
            return (x - mean) / (std + EPS) * gamma + beta
        key = jax.random.key(seed)
        ks = jax.random.split(key, 8)
        v = jax.random.normal(ks[0], (B, LK, D_MODEL), jnp.float32)
        k = jax.random.normal(ks[1], (B, LK, D_MODEL), jnp.float32)
        q = jax.random.normal(ks[2], (B, LQ, D_MODEL), jnp.float32)
        mask = jax.random.randint(ks[3], (B, LQ, LK), 0, 2).astype(bool)

        def xav(kk, shape):
            std = np.sqrt(2.0 / (shape[-2] + shape[-1]))
            return jax.random.normal(kk, shape, jnp.float32) * std
        w_q = xav(ks[4], (N_HEAD, D_MODEL, DQ))
        w_k = xav(ks[5], (N_HEAD, D_MODEL, DK))
        w_v = xav(ks[6], (N_HEAD, D_MODEL, DV))
        fan_in = N_HEAD * DV
        bound = 1.0 / np.sqrt(fan_in)
        kw, kb = jax.random.split(ks[7])
        w_o = jax.random.uniform(kw, (fan_in, D_MODEL), jnp.float32, -bound, bound)
        b_o = jax.random.uniform(kb, (D_MODEL,), jnp.float32, -bound, bound)
        gamma = jnp.ones((D_MODEL,), jnp.float32)
        beta = jnp.zeros((D_MODEL,), jnp.float32)
        return {'v': v, 'k': k, 'q': q, 'mask': mask, 'w_q': w_q, 'w_k': w_k, 'w_v': w_v, 'w_o': w_o, 'b_o': b_o, 'gamma': gamma, 'beta': beta}
    _L0_xattn_all = _L0_xattn_setup()
    _L0_xattn_in = {k: v for k, v in _L0_xattn_all.items() if k in ('w_q', 'w_k', 'w_v', 'w_o', 'b_o', 'gamma', 'beta')}
    del _L0_xattn_all

    def _L0_ffn_setup():
        import jax, jax.numpy as jnp
        import numpy as np
        H, F, E_SHARED, E_ROUTED, K = (256, 1024, 1, 8, 2)

        def _expert(x, w_up, w_down):
            h = jax.nn.gelu(jnp.einsum('bsh,hf->bsf', x, w_up), approximate=False)
            return jnp.einsum('bsf,fh->bsh', h, w_down)
        key = jax.random.key(seed)
        ks = jax.random.split(key, 6)
        x = jax.random.normal(ks[0], (4, 512, H), dtype=jnp.float32)
        s = 0.02
        shared_up = jax.random.normal(ks[1], (E_SHARED, H, F), dtype=jnp.float32) * s
        shared_down = jax.random.normal(ks[2], (E_SHARED, F, H), dtype=jnp.float32) * s
        routed_up = jax.random.normal(ks[3], (E_ROUTED, H, F), dtype=jnp.float32) * s
        routed_down = jax.random.normal(ks[4], (E_ROUTED, F, H), dtype=jnp.float32) * s
        router_w = jax.random.normal(ks[5], (H, E_ROUTED), dtype=jnp.float32) * s
        return {'x': x, 'shared_up': shared_up, 'shared_down': shared_down, 'routed_up': routed_up, 'routed_down': routed_down, 'router_w': router_w}
    _L0_ffn_all = _L0_ffn_setup()
    _L0_ffn_in = {k: v for k, v in _L0_ffn_all.items() if k in ('shared_up', 'shared_down', 'routed_up', 'routed_down', 'router_w')}
    del _L0_ffn_all

    def _L1_attn_setup():
        import jax, jax.numpy as jnp
        import numpy as np
        import math
        D_MODEL = 256
        N_HEADS = 16
        D_HEAD = D_MODEL // N_HEADS
        LSR_RANK = 32
        B, T = (4, 512)
        key = jax.random.key(seed)
        ks = jax.random.split(key, 11)
        s = 1.0 / math.sqrt(D_MODEL)
        x = jax.random.normal(ks[0], (B, T, D_MODEL), dtype=jnp.float32)
        Wq = jax.random.uniform(ks[1], (D_MODEL, D_MODEL), minval=-s, maxval=s)
        bq = jax.random.uniform(ks[2], (D_MODEL,), minval=-s, maxval=s)
        Wk = jax.random.uniform(ks[3], (D_MODEL, D_MODEL), minval=-s, maxval=s)
        bk = jax.random.uniform(ks[4], (D_MODEL,), minval=-s, maxval=s)
        Wv = jax.random.uniform(ks[5], (D_MODEL, D_MODEL), minval=-s, maxval=s)
        bv = jax.random.uniform(ks[6], (D_MODEL,), minval=-s, maxval=s)
        Wo = jax.random.uniform(ks[7], (D_MODEL, D_MODEL), minval=-s, maxval=s)
        bo = jax.random.uniform(ks[8], (D_MODEL,), minval=-s, maxval=s)
        Wq_lsr = jax.random.normal(ks[9], (N_HEADS, D_HEAD, LSR_RANK)) / math.sqrt(D_HEAD)
        Wk_lsr = jax.random.normal(ks[10], (N_HEADS, D_HEAD, LSR_RANK)) / math.sqrt(D_HEAD)
        return {'x': x, 'Wq': Wq, 'bq': bq, 'Wk': Wk, 'bk': bk, 'Wv': Wv, 'bv': bv, 'Wo': Wo, 'bo': bo, 'Wq_lsr': Wq_lsr, 'Wk_lsr': Wk_lsr}
    _L1_attn_all = _L1_attn_setup()
    _L1_attn_in = {k: v for k, v in _L1_attn_all.items() if k in ('Wq', 'bq', 'Wk', 'bk', 'Wv', 'bv', 'Wo', 'bo', 'Wq_lsr', 'Wk_lsr')}
    del _L1_attn_all

    def _L1_xattn_setup():
        import jax, jax.numpy as jnp
        import numpy as np
        SCALE_BASE = 512.0
        GN_EPS = 1e-05

        def _xpos(x, downscale):
            L, D = (x.shape[-2], x.shape[-1])
            half = D // 2
            base = (jnp.arange(0, D, 2, dtype=jnp.float32) + 0.4 * D) / (1.4 * D)
            min_pos = -(L // 2)
            power = (jnp.arange(min_pos, min_pos + L, dtype=jnp.float32) / SCALE_BASE)[:, None]
            scale = base[None, :] ** power
            inv_freq = 1.0 / 10000.0 ** (jnp.arange(half, dtype=jnp.float32) / half)
            ang = jnp.arange(L, dtype=jnp.float32)[:, None] * inv_freq[None, :]
            sin, cos = (jnp.sin(ang), jnp.cos(ang))
            if downscale:
                scale = 1.0 / scale
            sin_s = jnp.repeat(sin * scale, 2, axis=-1)
            cos_s = jnp.repeat(cos * scale, 2, axis=-1)
            x1, x2 = (x[..., ::2], x[..., 1::2])
            rot = jnp.stack((-x2, x1), axis=-1).reshape(x.shape)
            return x * cos_s + rot * sin_s

        def _decay_mask(L, H):
            gammas = 1.0 - jnp.exp(jnp.linspace(np.log(1.0 / 32.0), np.log(1.0 / 512.0), H)).astype(jnp.float32)
            idx = jnp.arange(L)
            dist = idx[:, None] - idx[None, :]
            causal = dist >= 0
            d = jnp.maximum(dist, 0).astype(jnp.float32)
            return jnp.where(causal[None], gammas[:, None, None] ** d[None], 0.0)
        key = jax.random.key(seed)
        ks = jax.random.split(key, 9)
        B, L, D, H = (2, 512, 256, 16)
        hd = D // H
        return {'query': jax.random.normal(ks[0], (B, L, D), jnp.float32), 'key': jax.random.normal(ks[1], (B, L, D), jnp.float32), 'value': jax.random.normal(ks[2], (B, L, D), jnp.float32), 'W_Q': jax.random.normal(ks[3], (H, D, hd), jnp.float32) / D, 'W_K': jax.random.normal(ks[4], (H, D, hd), jnp.float32) / D, 'W_V': jax.random.normal(ks[5], (H, D, hd), jnp.float32) / D, 'g_w': jax.random.normal(ks[6], (D, D), jnp.float32) * (2.0 / (D + D)) ** 0.5, 'g_b': jnp.zeros((D,), jnp.float32), 'out_w': jax.random.normal(ks[7], (D, D), jnp.float32) * (2.0 / (D + D)) ** 0.5, 'out_b': jnp.zeros((D,), jnp.float32)}
    _L1_xattn_all = _L1_xattn_setup()
    _L1_xattn_in = {k: v for k, v in _L1_xattn_all.items() if k in ('W_Q', 'W_K', 'W_V', 'g_w', 'g_b', 'out_w', 'out_b')}
    del _L1_xattn_all

    def _L1_ffn_setup():
        import jax, jax.numpy as jnp
        import numpy as np
        E = 8
        TOPK = 2
        PRIME = 11
        HASH_OFF = 7919
        N_SHARED = 1
        key = jax.random.key(seed)
        ks = jax.random.split(key, 8)
        B, T, C, Hs, Hr = (4, 2048, 256, 512, 256)
        sc = lambda k, shape, fan: jax.random.normal(k, shape, jnp.float32) * fan ** (-0.5)
        return {'x': jax.random.normal(ks[0], (B, T, C), jnp.float32), 't_emb': jax.random.normal(ks[1], (B, C), jnp.float32), 'sw1': sc(ks[2], (C, Hs), C), 'sb1': jnp.zeros((Hs,), jnp.float32), 'sw3': sc(ks[3], (C, Hs), C), 'sb3': jnp.zeros((Hs,), jnp.float32), 'sw2': sc(ks[4], (Hs, C), Hs), 'sb2': jnp.zeros((C,), jnp.float32), 'w1': sc(ks[5], (E, C, Hr), C), 'b1': jnp.zeros((E, Hr), jnp.float32), 'w2': sc(ks[6], (E, Hr, C), Hr), 'b2': jnp.zeros((E, C), jnp.float32)}
    _L1_ffn_all = _L1_ffn_setup()
    _L1_ffn_in = {k: v for k, v in _L1_ffn_all.items() if k in ('t_emb', 'sw1', 'sb1', 'sw3', 'sb3', 'sw2', 'sb2', 'w1', 'b1', 'w2', 'b2')}
    del _L1_ffn_all
    return {'x': x, 'ctx_1024': ctx_1024, 'mask_BxSxS2_bk1': mask_BxSxS2_bk1, 'L0_attn_fwd_in_proj_w': _L0_attn_in['fwd_in_proj_w'], 'L0_attn_fwd_conv_w': _L0_attn_in['fwd_conv_w'], 'L0_attn_fwd_conv_b': _L0_attn_in['fwd_conv_b'], 'L0_attn_fwd_x_proj_w': _L0_attn_in['fwd_x_proj_w'], 'L0_attn_fwd_dt_proj_w': _L0_attn_in['fwd_dt_proj_w'], 'L0_attn_fwd_dt_proj_b': _L0_attn_in['fwd_dt_proj_b'], 'L0_attn_fwd_A_log': _L0_attn_in['fwd_A_log'], 'L0_attn_fwd_D': _L0_attn_in['fwd_D'], 'L0_attn_fwd_out_proj_w': _L0_attn_in['fwd_out_proj_w'], 'L0_attn_bwd_in_proj_w': _L0_attn_in['bwd_in_proj_w'], 'L0_attn_bwd_conv_w': _L0_attn_in['bwd_conv_w'], 'L0_attn_bwd_conv_b': _L0_attn_in['bwd_conv_b'], 'L0_attn_bwd_x_proj_w': _L0_attn_in['bwd_x_proj_w'], 'L0_attn_bwd_dt_proj_w': _L0_attn_in['bwd_dt_proj_w'], 'L0_attn_bwd_dt_proj_b': _L0_attn_in['bwd_dt_proj_b'], 'L0_attn_bwd_A_log': _L0_attn_in['bwd_A_log'], 'L0_attn_bwd_D': _L0_attn_in['bwd_D'], 'L0_attn_bwd_out_proj_w': _L0_attn_in['bwd_out_proj_w'], 'L0_attn_ln_gamma': _L0_attn_in['ln_gamma'], 'L0_attn_ln_beta': _L0_attn_in['ln_beta'], 'L0_xattn_w_q': _L0_xattn_in['w_q'], 'L0_xattn_w_k': _L0_xattn_in['w_k'], 'L0_xattn_w_v': _L0_xattn_in['w_v'], 'L0_xattn_w_o': _L0_xattn_in['w_o'], 'L0_xattn_b_o': _L0_xattn_in['b_o'], 'L0_xattn_gamma': _L0_xattn_in['gamma'], 'L0_xattn_beta': _L0_xattn_in['beta'], 'L0_ffn_shared_up': _L0_ffn_in['shared_up'], 'L0_ffn_shared_down': _L0_ffn_in['shared_down'], 'L0_ffn_routed_up': _L0_ffn_in['routed_up'], 'L0_ffn_routed_down': _L0_ffn_in['routed_down'], 'L0_ffn_router_w': _L0_ffn_in['router_w'], 'L1_attn_Wq': _L1_attn_in['Wq'], 'L1_attn_bq': _L1_attn_in['bq'], 'L1_attn_Wk': _L1_attn_in['Wk'], 'L1_attn_bk': _L1_attn_in['bk'], 'L1_attn_Wv': _L1_attn_in['Wv'], 'L1_attn_bv': _L1_attn_in['bv'], 'L1_attn_Wo': _L1_attn_in['Wo'], 'L1_attn_bo': _L1_attn_in['bo'], 'L1_attn_Wq_lsr': _L1_attn_in['Wq_lsr'], 'L1_attn_Wk_lsr': _L1_attn_in['Wk_lsr'], 'L1_xattn_W_Q': _L1_xattn_in['W_Q'], 'L1_xattn_W_K': _L1_xattn_in['W_K'], 'L1_xattn_W_V': _L1_xattn_in['W_V'], 'L1_xattn_g_w': _L1_xattn_in['g_w'], 'L1_xattn_g_b': _L1_xattn_in['g_b'], 'L1_xattn_out_w': _L1_xattn_in['out_w'], 'L1_xattn_out_b': _L1_xattn_in['out_b'], 'L1_ffn_t_emb': _L1_ffn_in['t_emb'], 'L1_ffn_sw1': _L1_ffn_in['sw1'], 'L1_ffn_sb1': _L1_ffn_in['sb1'], 'L1_ffn_sw3': _L1_ffn_in['sw3'], 'L1_ffn_sb3': _L1_ffn_in['sb3'], 'L1_ffn_sw2': _L1_ffn_in['sw2'], 'L1_ffn_sb2': _L1_ffn_in['sb2'], 'L1_ffn_w1': _L1_ffn_in['w1'], 'L1_ffn_b1': _L1_ffn_in['b1'], 'L1_ffn_w2': _L1_ffn_in['w2'], 'L1_ffn_b2': _L1_ffn_in['b2']}

def reference(x, ctx_1024, mask_BxSxS2_bk1, L0_attn_fwd_in_proj_w, L0_attn_fwd_conv_w, L0_attn_fwd_conv_b, L0_attn_fwd_x_proj_w, L0_attn_fwd_dt_proj_w, L0_attn_fwd_dt_proj_b, L0_attn_fwd_A_log, L0_attn_fwd_D, L0_attn_fwd_out_proj_w, L0_attn_bwd_in_proj_w, L0_attn_bwd_conv_w, L0_attn_bwd_conv_b, L0_attn_bwd_x_proj_w, L0_attn_bwd_dt_proj_w, L0_attn_bwd_dt_proj_b, L0_attn_bwd_A_log, L0_attn_bwd_D, L0_attn_bwd_out_proj_w, L0_attn_ln_gamma, L0_attn_ln_beta, L0_xattn_w_q, L0_xattn_w_k, L0_xattn_w_v, L0_xattn_w_o, L0_xattn_b_o, L0_xattn_gamma, L0_xattn_beta, L0_ffn_shared_up, L0_ffn_shared_down, L0_ffn_routed_up, L0_ffn_routed_down, L0_ffn_router_w, L1_attn_Wq, L1_attn_bq, L1_attn_Wk, L1_attn_bk, L1_attn_Wv, L1_attn_bv, L1_attn_Wo, L1_attn_bo, L1_attn_Wq_lsr, L1_attn_Wk_lsr, L1_xattn_W_Q, L1_xattn_W_K, L1_xattn_W_V, L1_xattn_g_w, L1_xattn_g_b, L1_xattn_out_w, L1_xattn_out_b, L1_ffn_t_emb, L1_ffn_sw1, L1_ffn_sb1, L1_ffn_sw3, L1_ffn_sb3, L1_ffn_sw2, L1_ffn_sb2, L1_ffn_w1, L1_ffn_b1, L1_ffn_w2, L1_ffn_b2):
    import jax
    import jax.numpy as jnp

    def _L0_attn_ref(x, fwd_in_proj_w, fwd_conv_w, fwd_conv_b, fwd_x_proj_w, fwd_dt_proj_w, fwd_dt_proj_b, fwd_A_log, fwd_D, fwd_out_proj_w, bwd_in_proj_w, bwd_conv_w, bwd_conv_b, bwd_x_proj_w, bwd_dt_proj_w, bwd_dt_proj_b, bwd_A_log, bwd_D, bwd_out_proj_w, ln_gamma, ln_beta):
        import jax, jax.numpy as jnp
        import numpy as np
        from jax import lax
        B_, L_, D_MODEL = (2, 256, 256)
        D_STATE, D_CONV, EXPAND = (16, 4, 2)
        D_INNER = EXPAND * D_MODEL
        DT_RANK = (D_MODEL + 15) // 16
        LN_EPS = 1e-05

        def _silu(v):
            return v * jax.nn.sigmoid(v)

        def _mamba_params(key):
            ks = jax.random.split(key, 6)
            g = lambda k, shp, sc: jax.random.normal(k, shp, jnp.float32) * sc
            return {'in_proj_w': g(ks[0], (2 * D_INNER, D_MODEL), D_MODEL ** (-0.5)), 'conv_w': g(ks[1], (D_INNER, D_CONV), D_CONV ** (-0.5)), 'conv_b': jnp.zeros((D_INNER,), jnp.float32), 'x_proj_w': g(ks[2], (DT_RANK + 2 * D_STATE, D_INNER), D_INNER ** (-0.5)), 'dt_proj_w': g(ks[3], (D_INNER, DT_RANK), DT_RANK ** (-0.5)), 'dt_proj_b': jax.random.uniform(ks[4], (D_INNER,), jnp.float32, -4.0, -2.0), 'A_log': jnp.log(jnp.broadcast_to(jnp.arange(1, D_STATE + 1, dtype=jnp.float32), (D_INNER, D_STATE))), 'D': jnp.ones((D_INNER,), jnp.float32), 'out_proj_w': g(ks[5], (D_MODEL, D_INNER), D_INNER ** (-0.5))}

        def _mamba(x, in_proj_w, conv_w, conv_b, x_proj_w, dt_proj_w, dt_proj_b, A_log, D, out_proj_w):
            b, l, _ = x.shape
            xz = x @ in_proj_w.T
            xi, z = jnp.split(xz, 2, axis=-1)
            xp = jnp.pad(xi, ((0, 0), (D_CONV - 1, 0), (0, 0)))
            xc = conv_b + sum((xp[:, k:k + l, :] * conv_w[:, k] for k in range(D_CONV)))
            xc = _silu(xc)
            dbl = xc @ x_proj_w.T
            dt = jax.nn.softplus(dbl[..., :DT_RANK] @ dt_proj_w.T + dt_proj_b)
            Bm = dbl[..., DT_RANK:DT_RANK + D_STATE]
            Cm = dbl[..., DT_RANK + D_STATE:]
            A = -jnp.exp(A_log)
            dA = jnp.exp(dt[..., None] * A)
            dBu = (dt * xc)[..., None] * Bm[:, :, None, :]

            def step(h, inp):
                dA_t, dBu_t, C_t = inp
                h = dA_t * h + dBu_t
                return (h, jnp.einsum('bdn,bn->bd', h, C_t))
            h0 = jnp.zeros((b, D_INNER, D_STATE), x.dtype)
            _, ys = lax.scan(step, h0, (dA.transpose(1, 0, 2, 3), dBu.transpose(1, 0, 2, 3), Cm.transpose(1, 0, 2)))
            y = ys.transpose(1, 0, 2) + xc * D
            y = y * _silu(z)
            return y @ out_proj_w.T
        yf = _mamba(x, fwd_in_proj_w, fwd_conv_w, fwd_conv_b, fwd_x_proj_w, fwd_dt_proj_w, fwd_dt_proj_b, fwd_A_log, fwd_D, fwd_out_proj_w)
        yb = _mamba(jnp.flip(x, 1), bwd_in_proj_w, bwd_conv_w, bwd_conv_b, bwd_x_proj_w, bwd_dt_proj_w, bwd_dt_proj_b, bwd_A_log, bwd_D, bwd_out_proj_w)
        yo = yf + jnp.flip(yb, 1)
        mu = jnp.mean(yo, axis=-1, keepdims=True)
        var = jnp.mean(jnp.square(yo - mu), axis=-1, keepdims=True)
        return ln_gamma * (yo - mu) / jnp.sqrt(var + LN_EPS) + ln_beta

    def _L0_xattn_ref(v, k, q, mask, w_q, w_k, w_v, w_o, b_o, gamma, beta):
        import jax, jax.numpy as jnp
        import numpy as np
        N_HEAD, D_MODEL, DQ, DK, DV = (16, 256, 64, 64, 64)
        B, LQ, LK = (2, 512, 512)
        EPS = 0.001

        def _layer_norm(x, gamma, beta):
            mean = jnp.mean(x, axis=-1, keepdims=True)
            std = jnp.std(x, axis=-1, keepdims=True, ddof=1)
            return (x - mean) / (std + EPS) * gamma + beta
        residual = k
        qh = jnp.einsum('bld,hde->hble', q, w_q)
        kh = jnp.einsum('bld,hde->hble', k, w_k)
        vh = jnp.einsum('bld,hde->hble', v, w_v)
        scale = 1.0 / np.sqrt(DK)
        scores = jnp.einsum('hbqe,hbke->hbqk', qh, kh) * scale
        scores = jnp.where(mask[None], -jnp.inf, scores)
        attn = jax.nn.softmax(scores, axis=-1)
        out = jnp.einsum('hbqk,hbke->hbqe', attn, vh)
        out = out.transpose(1, 2, 0, 3).reshape(out.shape[1], out.shape[2], -1)
        out = out @ w_o + b_o
        x = out + residual
        return _layer_norm(x, gamma, beta)

    def _L0_ffn_ref(x, shared_up, shared_down, routed_up, routed_down, router_w):
        import jax, jax.numpy as jnp
        import numpy as np
        H, F, E_SHARED, E_ROUTED, K = (256, 1024, 1, 8, 2)

        def _expert(x, w_up, w_down):
            h = jax.nn.gelu(jnp.einsum('bsh,hf->bsf', x, w_up), approximate=False)
            return jnp.einsum('bsf,fh->bsh', h, w_down)
        shared_out = jnp.zeros_like(x)
        for i in range(E_SHARED):
            shared_out = shared_out + _expert(x, shared_up[i], shared_down[i])
        probs = jax.nn.softmax(jnp.einsum('bsh,he->bse', x, router_w), axis=-1)
        top_k_prob, top_k_idx = jax.lax.top_k(probs, K)
        onehot = jax.nn.one_hot(top_k_idx, E_ROUTED, dtype=x.dtype)
        gates = jnp.einsum('bsk,bske->bse', top_k_prob, onehot)
        routed_out = jnp.zeros_like(x)
        for e in range(E_ROUTED):
            y = _expert(x, routed_up[e], routed_down[e])
            routed_out = routed_out + gates[..., e:e + 1] * y
        return shared_out + routed_out + x

    def _L1_attn_ref(x, Wq, bq, Wk, bk, Wv, bv, Wo, bo, Wq_lsr, Wk_lsr):
        import jax, jax.numpy as jnp
        import numpy as np
        import math
        D_MODEL = 256
        N_HEADS = 16
        D_HEAD = D_MODEL // N_HEADS
        LSR_RANK = 32
        B, T = (4, 512)
        Bq, Tq, _ = x.shape

        def split_heads(y):
            return y.reshape(Bq, Tq, N_HEADS, D_HEAD).transpose(0, 2, 1, 3)
        q = split_heads(x @ Wq.T + bq)
        k = split_heads(x @ Wk.T + bk)
        v = split_heads(x @ Wv.T + bv)
        q_lr = jnp.einsum('bhtd,hdr->bhtr', q, Wq_lsr)
        k_lr = jnp.einsum('bhtd,hdr->bhtr', k, Wk_lsr)
        scale = 1.0 / math.sqrt(max(LSR_RANK, 1))
        scores = jnp.einsum('bhir,bhjr->bhij', q_lr, k_lr) * scale
        causal_mask = jnp.triu(jnp.ones((Tq, Tq), dtype=bool), k=1)
        scores = jnp.where(causal_mask, jnp.float32(-jnp.inf), scores)
        attn = jax.nn.softmax(scores, axis=-1)
        y = jnp.einsum('bhij,bhjd->bhid', attn, v)
        y = y.transpose(0, 2, 1, 3).reshape(Bq, Tq, D_MODEL)
        return y @ Wo.T + bo

    def _L1_xattn_ref(query, key, value, W_Q, W_K, W_V, g_w, g_b, out_w, out_b):
        import jax, jax.numpy as jnp
        import numpy as np
        SCALE_BASE = 512.0
        GN_EPS = 1e-05

        def _xpos(x, downscale):
            L, D = (x.shape[-2], x.shape[-1])
            half = D // 2
            base = (jnp.arange(0, D, 2, dtype=jnp.float32) + 0.4 * D) / (1.4 * D)
            min_pos = -(L // 2)
            power = (jnp.arange(min_pos, min_pos + L, dtype=jnp.float32) / SCALE_BASE)[:, None]
            scale = base[None, :] ** power
            inv_freq = 1.0 / 10000.0 ** (jnp.arange(half, dtype=jnp.float32) / half)
            ang = jnp.arange(L, dtype=jnp.float32)[:, None] * inv_freq[None, :]
            sin, cos = (jnp.sin(ang), jnp.cos(ang))
            if downscale:
                scale = 1.0 / scale
            sin_s = jnp.repeat(sin * scale, 2, axis=-1)
            cos_s = jnp.repeat(cos * scale, 2, axis=-1)
            x1, x2 = (x[..., ::2], x[..., 1::2])
            rot = jnp.stack((-x2, x1), axis=-1).reshape(x.shape)
            return x * cos_s + rot * sin_s

        def _decay_mask(L, H):
            gammas = 1.0 - jnp.exp(jnp.linspace(np.log(1.0 / 32.0), np.log(1.0 / 512.0), H)).astype(jnp.float32)
            idx = jnp.arange(L)
            dist = idx[:, None] - idx[None, :]
            causal = dist >= 0
            d = jnp.maximum(dist, 0).astype(jnp.float32)
            return jnp.where(causal[None], gammas[:, None, None] ** d[None], 0.0)
        B, L, D = query.shape
        H = W_Q.shape[0]
        q = jnp.einsum('bld,hde->bhle', query, W_Q)
        k = jnp.einsum('bld,hde->bhle', key, W_K)
        v = jnp.einsum('bld,hde->bhle', value, W_V)
        q = _xpos(q, downscale=False)
        k = _xpos(k, downscale=True)
        sim = jnp.einsum('bhnd,bhsd->bhns', q, k) * _decay_mask(L, H)[None]
        ret = jnp.einsum('bhns,bhsd->bhnd', sim, v)
        mu = ret.mean(axis=-1, keepdims=True)
        var = ret.var(axis=-1, keepdims=True)
        ret = (ret - mu) / jnp.sqrt(var + GN_EPS)
        ret = ret.transpose(0, 2, 1, 3).reshape(B, L, D)
        gate = jax.nn.silu(query @ g_w.T + g_b)
        return ret * gate @ out_w.T + out_b

    def _L1_ffn_ref(x, t_emb, sw1, sb1, sw3, sb3, sw2, sb2, w1, b1, w2, b2):
        import jax, jax.numpy as jnp
        import numpy as np
        E = 8
        TOPK = 2
        PRIME = 11
        HASH_OFF = 7919
        N_SHARED = 1
        B, T, C = x.shape
        N = B * T
        xf = x.reshape(N, C)
        shared = jax.nn.silu(xf @ sw1 + sb1) * (xf @ sw3 + sb3) @ sw2 + sb2
        tok = jnp.arange(N)
        out = jnp.zeros((N, C), x.dtype)
        for k in range(TOPK):
            exp_ids = (tok * PRIME + k * HASH_OFF) % E
            sort_idx = jnp.argsort(exp_ids)
            xs = xf[sort_idx].reshape(E, N // E, C)
            h = jax.nn.gelu(jnp.einsum('enc,ech->enh', xs, w1) + b1[:, None, :], approximate=False)
            y = jnp.einsum('enh,ehc->enc', h, w2) + b2[:, None, :]
            out = out.at[sort_idx].add(y.reshape(N, C))
        out = out / TOPK
        return ((shared + out) / (N_SHARED + 1)).reshape(B, T, C)
    x = _layernorm(x + _L0_attn_ref(x, L0_attn_fwd_in_proj_w, L0_attn_fwd_conv_w, L0_attn_fwd_conv_b, L0_attn_fwd_x_proj_w, L0_attn_fwd_dt_proj_w, L0_attn_fwd_dt_proj_b, L0_attn_fwd_A_log, L0_attn_fwd_D, L0_attn_fwd_out_proj_w, L0_attn_bwd_in_proj_w, L0_attn_bwd_conv_w, L0_attn_bwd_conv_b, L0_attn_bwd_x_proj_w, L0_attn_bwd_dt_proj_w, L0_attn_bwd_dt_proj_b, L0_attn_bwd_A_log, L0_attn_bwd_D, L0_attn_bwd_out_proj_w, L0_attn_ln_gamma, L0_attn_ln_beta), axis=-1)
    x = _layernorm(x + _L0_xattn_ref(ctx_1024, ctx_1024, x, mask_BxSxS2_bk1, L0_xattn_w_q, L0_xattn_w_k, L0_xattn_w_v, L0_xattn_w_o, L0_xattn_b_o, L0_xattn_gamma, L0_xattn_beta), axis=-1)
    x = _layernorm(x + _L0_ffn_ref(x, L0_ffn_shared_up, L0_ffn_shared_down, L0_ffn_routed_up, L0_ffn_routed_down, L0_ffn_router_w), axis=-1)
    x = _layernorm(x + _L1_attn_ref(x, L1_attn_Wq, L1_attn_bq, L1_attn_Wk, L1_attn_bk, L1_attn_Wv, L1_attn_bv, L1_attn_Wo, L1_attn_bo, L1_attn_Wq_lsr, L1_attn_Wk_lsr), axis=-1)
    x = _layernorm(x + _L1_xattn_ref(x, ctx_1024, ctx_1024, L1_xattn_W_Q, L1_xattn_W_K, L1_xattn_W_V, L1_xattn_g_w, L1_xattn_g_b, L1_xattn_out_w, L1_xattn_out_b), axis=-1)
    x = _layernorm(x + _L1_ffn_ref(x, L1_ffn_t_emb, L1_ffn_sw1, L1_ffn_sb1, L1_ffn_sw3, L1_ffn_sb3, L1_ffn_sw2, L1_ffn_sb2, L1_ffn_w1, L1_ffn_b1, L1_ffn_w2, L1_ffn_b2), axis=-1)
    return x

_drawn_inputs = setup_inputs


def setup_inputs(seed=0):
    import zlib

    import numpy as np

    out = dict(_drawn_inputs(seed))
    spreads = {'L0_attn_fwd_conv_b': (0.0, 0.1),
     'L0_attn_fwd_D': (1.0, 0.2),
     'L0_attn_bwd_conv_b': (0.0, 0.1),
     'L0_attn_bwd_D': (1.0, 0.2),
     'L0_attn_ln_gamma': (1.0, 0.2),
     'L0_attn_ln_beta': (0.0, 0.1),
     'L0_xattn_gamma': (1.0, 0.2),
     'L0_xattn_beta': (0.0, 0.1),
     'L1_xattn_g_b': (0.0, 0.1),
     'L1_xattn_out_b': (0.0, 0.1),
     'L1_ffn_sb1': (0.0, 0.283),
     'L1_ffn_sb3': (0.0, 0.297),
     'L1_ffn_sb2': (0.0, 0.1),
     'L1_ffn_b1': (0.0, 0.35),
     'L1_ffn_b2': (0.0, 0.1)}
    factors = {'L0_xattn_b_o': 3.722,
     'L0_ffn_routed_up': 3.513,
     'L0_ffn_routed_down': 3.411,
     'L0_ffn_router_w': 3.837,
     'L1_attn_Wq': 3.547,
     'L1_attn_bq': 8.0,
     'L1_attn_Wk': 3.542,
     'L1_attn_bk': 8.0,
     'L1_attn_Wq_lsr': 3.528,
     'L1_attn_Wk_lsr': 3.582}
    for name, (base, spread) in spreads.items():
        noise = np.random.default_rng([zlib.crc32(name.encode()), seed]).standard_normal(out[name].shape)
        drawn = base * np.exp(spread * noise) if base else spread * noise
        out[name] = jnp.asarray(drawn.astype(out[name].dtype))
    for name, factor in factors.items():
        out[name] = (out[name] * factor).astype(out[name].dtype)
    return out
```

```python
from contextlib import ExitStack

import concourse.bass as bass
import numpy as np
from concourse import mybir

F32 = mybir.dt.float32
U8 = mybir.dt.uint8
ALU = mybir.AluOpType
ACT = mybir.ActivationFunctionType
AX_X = mybir.AxisListType.X

P = 128
NB, L, D = 4, 512, 256
TOK = NB * L
NT = TOK // P
LT = L // P
KD = D // P
DI, NS, DTR = 512, 16, 16
NJ = DI // P
DBL = DTR + 2 * NS
NQ = 4


def mamba_stage(nc, d, yo_dram, bc_dram):
    with ExitStack() as ctx:
        sb = lambda name, shape, dt=F32: ctx.enter_context(nc.sbuf_tensor("m_" + name, shape, dt))
        ps = lambda name, shape: ctx.enter_context(nc.psum_tensor("m_" + name, shape, F32))
        sem = lambda name: nc.alloc_semaphore("m_" + name)

        xT = sb("xT", [P, KD, L])
        in_w = sb("in_w", [P, 2, KD, 2 * DI])
        xp_w = sb("xp_w", [P, 2, NJ, DBL])
        dt_w = sb("dt_w", [DTR, 2, DI])
        out_w = sb("out_w", [P, 2, NJ, D])
        ident = sb("ident", [P, P])
        small = sb("small", [P, 2, NJ, 7])
        a_neg = sb("a_neg", [P, 2, NJ, NS])
        xi = sb("xi", [P, NJ, L + 6])
        xc = sb("xc", [P, 2, NJ, L])
        gz = sb("gz", [P, 2, NJ, L])
        dt = sb("dt", [P, 2, NJ, L])
        dv = sb("dv", [P, NJ, L])
        de = sb("de", [P, NJ, L])
        dbl = sb("dbl", [DBL, 2, L])
        bc = sb("bc", [P, 2, 2, NQ, L])
        da = sb("da", [P, 2, 2, NQ, L])
        h = sb("h", [P, 2, NQ, L])
        dtx = sb("dtx", [P, NJ, L])
        ys = sb("ys", [P, LT, D])

        rot = ps("rot", [P, 2, L])
        psy = ps("psy", [P, NJ, L])
        pso = ps("pso", [P, LT, D])

        loaded = sem("loaded")
        x_loaded = sem("x_loaded")
        zeroed = sem("zeroed")
        a_ready = sem("a_ready")
        rot_full = sem("rot_full")
        rot_free = sem("rot_free")
        conv_tap = sem("conv_tap")
        conv_done = sem("conv_done")
        xc_ready = sem("xc_ready")
        act_step = sem("act_step")
        dt_log = sem("dt_log")
        dt_ready = sem("dt_ready")
        dtx_ready = sem("dtx_ready")
        bc_stored = sem("bc_stored")
        bc_full = [sem(f"bc_full{s}") for s in range(2)]
        da_full = sem("da_full")
        dbu_ready = sem("dbu_ready")
        scanned = sem("scanned")
        p_ready = sem("p_ready")
        summed = sem("summed")
        y_plus = sem("y_plus")
        y_gated = sem("y_gated")
        o_full = sem("o_full")
        o_free = sem("o_free")
        ys_stored = sem("ys_stored")
        ys_free = sem("ys_free")
        QN = NS // NQ * NJ
        ROT = 2 * NJ + 1 + NJ
        LOADS = 9

        def passes(eng, a, b_, c, quantum, post):
            def one(b, u, last=False):
                nxt = (b, 1) if u == 0 else (b + 1, 0)
                for part, step in enumerate((a, b_, c, None)):
                    for q in range(part * NJ, (part + 1) * NJ):
                        quantum(b, u, q)
                    if step and not last:
                        step(*nxt)
                post(b, u)

            a(0, 0)
            b_(0, 0)
            c(0, 0)
            with eng.Fori(0, NB - 1) as b:
                one(b, 0)
                one(b, 1)
            one(NB - 1, 0)
            one(NB - 1, 1, last=True)

        with nc.Block() as block:
            @block.sync
            def _(sp):
                for dst, src in ((in_w[:, 0], d["in_w"][:, 0]), (ident[:], d["ident"]), (small[:], d["small"]),
                                 (a_neg[:], d["a_log"]), (xp_w[:], d["xp_w"]), (dt_w[:], d["dt_w"]),
                                 (in_w[:, 1], d["in_w"][:, 1]), (out_w[:, 0], d["out_w"][:, 0]),
                                 (out_w[:, 1], d["out_w"][:, 1])):
                    sp.dma_start(dst, src).then_inc(loaded, 16)
                with sp.Fori(0, NB) as b:
                    for u in range(2):
                        i = 2 * b + u
                        sp.wait_ge(rot_free, i * ROT + 2 * NJ + 1 + 2)
                        sp.dma_start(bc_dram[b, u], dbl[DTR:DBL, u, :]).then_inc(bc_stored, 16)
                        sp.wait_ge(bc_stored, 16 * i + 16)
                        for q in range(NS // NQ):
                            sp.wait_ge(p_ready, (i * (NS // NQ) + q + 1) * NJ)
                            src = bc_dram[b, u].rearrange("(c n) t -> c n t", c=2)[:, q * NQ:(q + 1) * NQ, :]
                            sp.dma_start(bc[:, q % 2], src.partition_broadcast(P)).then_inc(bc_full[q % 2], 16)

            @block.gpsimd
            def _(pool):
                pool.memset(xi[:, :, 0:3], 0.0).then_inc(zeroed, 1)
                pool.memset(xi[:, :, L + 3:L + 6], 0.0).then_inc(zeroed, 1)
                pool.memset(da[:, 0, :, :, 0:1], 0.0).then_inc(zeroed, 1)
                pool.memset(da[:, 1, :, :, L - 1:L], 0.0).then_inc(zeroed, 1)
                pool.nop().then_inc(ys_free, 1)

                def load_x(b):
                    pool.wait_ge(rot_full, 2 * b * ROT + 2 * NJ)
                    pool.dma_start(xT[:], d["xT"][:, :, bass.ts(b, L)]).then_inc(x_loaded, 16)

                def store_y(b):
                    pool.wait_ge(o_free, 2 * b + 2 + 2)
                    pool.dma_start(yo_dram.rearrange("(b t p) c -> b p t c", p=P, t=LT)[b], ys[:]).then_inc(ys_stored, 16)
                    pool.wait_ge(ys_stored, 16 * b + 16)
                    pool.nop().then_inc(ys_free, 1)

                load_x(0)
                with pool.Fori(0, NB - 1) as b:
                    load_x(b + 1)
                    store_y(b)
                store_y(NB - 1)

            @block.tensor
            def _(pe):
                pe.nop().then_inc(rot_full, ROT)
                pe.nop().then_inc(summed, 2)
                pe.wait_ge(loaded, LOADS * 16)

                def slot(b, u, k):
                    pe.wait_ge(rot_free, (2 * b + u) * ROT + k + 1)
                    return rot[:, (ROT * u + k) % 2, :]

                def in_proj(b, u):
                    pe.wait_ge(x_loaded, 16 * b + 16)
                    for m in range(2 * NJ):
                        out = slot(b, u, m)
                        for k in range(KD):
                            mm = pe.matmul(out, in_w[:, u, k, m * P:(m + 1) * P], xT[:, k, :],
                                           start=(k == 0), stop=(k == KD - 1))
                        mm.then_inc(rot_full, 1)

                def x_proj(b, u):
                    out = slot(b, u, 2 * NJ)
                    for j in range(NJ):
                        pe.wait_ge(xc_ready, (2 * b + u) * NJ + j + 1)
                        mm = pe.matmul(out[0:DBL], xp_w[:, u, j, :], xc[:, u, j, :], start=(j == 0), stop=(j == NJ - 1))
                    mm.then_inc(rot_full, 1)

                def dt_proj(b, u):
                    for j in range(NJ):
                        out = slot(b, u, 2 * NJ + 1 + j)
                        if j == 0:
                            pe.wait_ge(rot_free, (2 * b + u) * ROT + 2 * NJ + 1 + 2)
                        pe.matmul(out, dt_w[:, u, j * P:(j + 1) * P], dbl[0:DTR, u, :],
                                  start=True, stop=True).then_inc(rot_full, 1)

                def quantum(b, u, q):
                    i = 2 * b + u
                    if q < NJ:
                        pe.wait_ge(y_gated, i * NJ + q + 1)
                    pe.wait_ge(p_ready, i * QN + q + 1 + 2 * NJ)
                    for n in range(NQ):
                        mm = pe.matmul(psy[:, q % NJ, :], ident[:], h[:, q % 2, n, :],
                                       start=(q < NJ and n == 0), stop=(q >= QN - NJ and n == NQ - 1))
                    mm.then_inc(summed, 1)

                def post(b, u):
                    i = 2 * b + u
                    pe.wait_ge(o_free, i + 2)
                    pe.wait_ge(y_gated, (i + 1) * NJ + NJ)
                    for t in range(LT):
                        for j in range(NJ):
                            mm = pe.matmul(pso[:, t, :], gz[:, u, j, t * P:(t + 1) * P], out_w[:, u, j, :],
                                           start=(j == 0), stop=(j == NJ - 1))
                    mm.then_inc(o_full, 1)

                passes(pe, in_proj, x_proj, dt_proj, quantum, post)

            @block.scalar
            def _(act):
                act.nop().then_inc(rot_free, 2)
                act.wait_ge(loaded, LOADS * 16)
                act.wait_ge(zeroed, 4)
                act.activation(a_neg[:], a_neg[:], ACT.Exp).then_inc(a_ready, 1)
                act.wait_ge(a_ready, 1)
                act.mul(a_neg[:], a_neg[:], -1.0).then_inc(a_ready, 1)
                act.wait_ge(a_ready, 2)

                def slot(b, u, k):
                    act.wait_ge(rot_full, (2 * b + u) * ROT + k + 1 + ROT)
                    return rot[:, (ROT * u + k) % 2, :]

                def step_a(b, u):
                    i = 2 * b + u
                    for j in range(NJ):
                        act.wait_ge(conv_done, i * NJ + j + 1)
                        act.copy(xi[:, j, 3:3 + L], slot(b, u, j)).then_inc(rot_free, 1)
                    act.wait_ge(o_free, i + 1)
                    for j in range(NJ):
                        act.activation(gz[:, u, j, :], slot(b, u, NJ + j), ACT.Silu).then_inc(rot_free, 1)
                    for j in range(NJ):
                        act.wait_ge(conv_done, i * NJ + j + 1 + NJ)
                        act.activation(xc[:, u, j, :], dv[:, j, :], ACT.Silu).then_inc(xc_ready, 1)

                def step_b(b, u):
                    act.copy(dbl[:, u, :], slot(b, u, 2 * NJ)[0:DBL]).then_inc(rot_free, 1)

                def step_c(b, u):
                    i = 2 * b + u
                    for j in range(NJ):
                        act.activation(dv[:, j, :], slot(b, u, 2 * NJ + 1 + j), ACT.Identity,
                                       bias=small[:, u, j, 5:6]).then_inc(rot_free, 1)
                    act.wait_ge(rot_free, i * ROT + ROT + 2)
                    act.activation(de[:], dv[:], ACT.Abs).then_inc(act_step, 1)
                    act.wait_ge(act_step, 2 * i + 1)
                    act.activation(de[:], de[:], ACT.Exp, scale=-1.0).then_inc(act_step, 1)
                    act.wait_ge(act_step, 2 * i + 2)
                    act.activation(de[:], de[:], ACT.Ln, bias=1.0).then_inc(dt_log, 1)

                def quantum(b, u, q):
                    i = 2 * b + u
                    if q == 0:
                        act.wait_ge(dt_ready, i + 1)
                    act.wait_ge(scanned, i * QN + q + 1)
                    j, n0, at = q % NJ, q // NJ * NQ, 1 - u
                    for n in range(NQ):
                        e = act.activation(da[:, u, q % 2, n, at:at + L - 1], dt[:, u, j, at:at + L - 1], ACT.Exp,
                                           scale=a_neg[:, u, j, n0 + n:n0 + n + 1])
                    e.then_inc(da_full, 1)

                passes(act, step_a, step_b, step_c, quantum, lambda b, u: None)

            @block.vector
            def _(dve):
                dve.nop().then_inc(conv_done, NJ)
                dve.nop().then_inc(scanned, 2)
                dve.nop().then_inc(p_ready, 2 * NJ)
                dve.nop().then_inc(y_gated, NJ)
                dve.nop().then_inc(o_free, 2)
                dve.wait_ge(loaded, LOADS * 16)
                dve.wait_ge(zeroed, 4)

                def conv(b, u):
                    i = 2 * b + u
                    for k in range(4):
                        for j in range(NJ):
                            at = k if u == 0 else 6 - k
                            src, w = xi[:, j, at:at + L], small[:, u, j, k:k + 1]
                            if k == 0:
                                dve.wait_ge(rot_free, i * ROT + j + 1 + 2)
                                dve.tensor_scalar(dv[:, j, :], src, w, small[:, u, j, 4:5],
                                                  ALU.mult, ALU.add).then_inc(conv_tap, 1)
                                continue
                            dve.wait_ge(conv_tap, i * 3 * NJ + (k - 1) * NJ + j + 1)
                            dve.scalar_tensor_tensor(dv[:, j, :], src, w, dv[:, j, :], ALU.mult, ALU.add)\
                               .then_inc(conv_tap if k < 3 else conv_done, 1)

                def softplus(b, u):
                    dve.wait_ge(dt_log, 2 * b + u + 1)
                    dve.scalar_tensor_tensor(dt[:, u], dv[:], 0.0, de[:], ALU.max, ALU.add).then_inc(dt_ready, 1)

                def quantum(b, u, q):
                    i = 2 * b + u
                    n = i * QN + q
                    j, s = q % NJ, q // NJ
                    if q == 0:
                        dve.wait_ge(dt_ready, i + 1)
                        dve.wait_ge(xc_ready, i * NJ + NJ)
                        dve.tensor_tensor(dtx[:], dt[:, u], xc[:, u], ALU.mult).then_inc(dtx_ready, 1)
                        dve.wait_ge(dtx_ready, i + 1)
                    if j == 0:
                        dve.wait_ge(bc_full[s % 2], 32 * i + 16 * (s // 2) + 16)
                    dve.wait_ge(summed, n + 1)
                    hq = h[:, q % 2]
                    dve.tensor_tensor(hq, dtx[:, j:j + 1, :].broadcast_to([P, NQ, L]), bc[:, s % 2, 0],
                                      ALU.mult).then_inc(dbu_ready, 1)
                    dve.wait_ge(dbu_ready, n + 1)
                    dve.wait_ge(da_full, n + 1)
                    step = 1 if u == 0 else -1
                    flat = hq.rearrange("p n t -> p (n t)")[:, ::step]
                    decay = da[:, u, q % 2].rearrange("p n t -> p (n t)")[:, ::step]
                    dve.tensor_tensor_scan(flat, decay, flat, 0.0, ALU.mult, ALU.add).then_inc(scanned, 1)
                    dve.wait_ge(scanned, n + 1 + 2)
                    dve.tensor_tensor(hq, hq, bc[:, s % 2, 1], ALU.mult).then_inc(p_ready, 1)

                def post(b, u):
                    i = 2 * b + u
                    for j in range(NJ):
                        dve.wait_ge(summed, i * QN + QN - NJ + j + 1 + 2)
                        dve.scalar_tensor_tensor(de[:, j, :], xc[:, u, j, :], small[:, u, j, 6:7], psy[:, j, :],
                                                 ALU.mult, ALU.add).then_inc(y_plus, 1)
                    for j in range(NJ):
                        dve.wait_ge(y_plus, i * NJ + j + 1)
                        dve.tensor_tensor(gz[:, u, j, :], gz[:, u, j, :], de[:, j, :], ALU.mult).then_inc(y_gated, 1)
                    dve.wait_ge(o_full, i + 1)
                    if u == 0:
                        dve.wait_ge(ys_free, b + 1)
                        dve.tensor_copy(ys[:], pso[:]).then_inc(o_free, 1)
                    else:
                        dve.wait_ge(o_free, i + 2)
                        dve.tensor_tensor(ys[:], ys[:], pso[:], ALU.add).then_inc(o_free, 1)

                passes(dve, conv, lambda b, u: None, softplus, quantum, post)


def norm_stage(nc, name, x, xT, ident_dram, first=None, out=None):
    with ExitStack() as ctx:
        sb = lambda n, shape, dt=F32: ctx.enter_context(nc.sbuf_tensor(name + n, shape, dt))
        used = []

        def sem(n):
            used.append(nc.alloc_semaphore(name + n))
            return used[-1]

        ident = sb("ident", [P, P])
        eps = sb("eps", [P, 1])
        stat = sb("stat", [P, LT, 6])
        mv = sb("mv", [P, 2, LT, 2])
        rstd = sb("rstd", [P, 2, LT])
        if first:
            yo = sb("yo", [P, NT, D])
            gb = sb("gb", [P, 2, D])
        psT = ctx.enter_context(nc.psum_tensor(name + "psT", [P, 2, KD, L], F32))
        loaded = sem("loaded")
        step = sem("step")
        var_ready = sem("var_ready")
        std_ready = sem("std_ready")
        normed = sem("normed")
        turned = sem("turned")
        copied = sem("copied")
        stored = sem("stored")
        eps_ready = sem("eps_ready")
        ROUNDS = 2 if first else 1
        LOADS = 4 if first else 1

        with nc.Block() as block:
            @block.sync
            def _(sp):
                sp.dma_start(ident[:], ident_dram).then_inc(loaded, 16)
                if first:
                    sp.dma_start(yo[:], first["yo"].rearrange("(t p) c -> p t c", p=P)).then_inc(loaded, 16)
                    sp.dma_start(x[:], first["x"].rearrange("(t p) c -> p t c", p=P)).then_inc(loaded, 16)
                    sp.dma_start(gb[:], first["gb"].partition_broadcast(P)).then_inc(loaded, 16)
                if out is not None:
                    rows = out.rearrange("(b t p) c -> b p t c", p=P, t=LT)
                    for b in range(NB):
                        sp.wait_ge(normed, LT * (b + 1))
                        sp.dma_start(rows[b], x[:, LT * b:LT * (b + 1), :]).then_inc(stored, 16)
                    sp.wait_ge(stored, 16 * NB)

            @block.gpsimd
            def _(pool):
                pool.memset(eps[:], 1e-5).then_inc(eps_ready, 1)

            @block.vector
            def _(dve):
                dve.wait_ge(loaded, 16 * LOADS)
                steps = [0]

                def link(ins):
                    steps[0] += 1
                    ins.then_inc(step, 1)
                    dve.wait_ge(step, steps[0])

                def norm(rows, n, last):
                    for t in range(LT):
                        link(dve.bn_stats(stat[:, t, :], rows[:, t, :]))
                        ins = dve.bn_aggr(mv[:, n % 2, t, :], stat[:, t, :])
                    ins.then_inc(var_ready, 1)
                    dve.wait_ge(std_ready, n + 1)
                    link(dve.reciprocal(rstd[:, n % 2, :], rstd[:, n % 2, :]))
                    for t in range(LT):
                        ins = dve.tensor_scalar(rows[:, t, :], rows[:, t, :], mv[:, n % 2, t, 0:1],
                                                rstd[:, n % 2, t:t + 1], ALU.subtract, ALU.mult)
                        if last:
                            ins.then_inc(normed, 1)
                        elif t == LT - 1:
                            link(ins)

                for b in range(NB):
                    xs = x[:, LT * b:LT * (b + 1), :]
                    if first:
                        ys = yo[:, LT * b:LT * (b + 1), :]
                        norm(ys, 2 * b, False)
                        link(dve.tensor_tensor(ys, ys, gb[:, 0:1, :].broadcast_to([P, LT, D]), ALU.mult))
                        link(dve.tensor_tensor(ys, ys, gb[:, 1:2, :].broadcast_to([P, LT, D]), ALU.add))
                        link(dve.tensor_tensor(xs, xs, ys, ALU.add))
                    norm(xs, ROUNDS * (b + 1) - 1, True)

            def copy_out(act, b):
                for k in range(KD):
                    act.wait_ge(turned, KD * b + k + 1)
                    act.copy(xT[:, k, b * L:(b + 1) * L], psT[:, b % 2, k, :]).then_inc(copied, 1)

            @block.scalar
            def _(act):
                act.wait_ge(eps_ready, 1)
                for b in range(NB):
                    for r in range(ROUNDS):
                        n = ROUNDS * b + r
                        act.wait_ge(var_ready, n + 1)
                        act.activation(rstd[:, n % 2, :], mv[:, n % 2, :, 1], ACT.Sqrt, bias=eps[:]).then_inc(std_ready, 1)
                    if out is None and b >= 1:
                        copy_out(act, b - 1)
                if out is None:
                    copy_out(act, NB - 1)

            if out is None:
                @block.tensor
                def _(pe):
                    pe.wait_ge(loaded, 16 * LOADS)
                    for b in range(NB):
                        pe.wait_ge(normed, LT * (b + 1))
                        if b >= 2:
                            pe.wait_ge(copied, KD * (b - 1))
                        for k in range(KD):
                            for t in range(LT):
                                mm = pe.transpose(psT[:, b % 2, k, t * P:(t + 1) * P],
                                                  x[:, LT * b + t, k * P:(k + 1) * P], ident[:])
                            mm.then_inc(turned, 1)
        nc.clear_and_free_semaphores(used)
        nc.all_engine_barrier()


def cross_attention_stage(nc, d, x, xT):
    NH, HD = 16, 64
    NM = NH * HD // P
    with ExitStack() as ctx:
        sb = lambda name, shape, dt=F32: ctx.enter_context(nc.sbuf_tensor("c_" + name, shape, dt))
        ps = lambda name, shape: ctx.enter_context(nc.psum_tensor("c_" + name, shape, F32))
        sem = lambda name: nc.alloc_semaphore("c_" + name)

        ident = sb("ident", [P, P])
        wq = sb("wq", [P, KD, NH * HD])
        wk = sb("wk", [P, KD, NH * HD])
        wv = sb("wv", [P, KD, NH * HD])
        wo = sb("wo", [P, NM, D])
        rows = sb("rows", [P, 3, D])
        ctxT = sb("ctxT", [P, KD, L])
        res = sb("res", [P, LT, D])
        mask = sb("mask", [P, LT, L], U8)
        bias = sb("bias", [P, LT, L])
        kT = sb("kT", [P, NM, L])
        qT = sb("qT", [P, NM, L])
        v = sb("v", [P, LT, NH * HD])
        pr = sb("pr", [P, 3, LT, L])
        pT = sb("pT", [P, 2, LT, L])
        o = sb("o", [P, LT, NH * HD])
        oT = sb("oT", [P, NM, L])
        mx = sb("mx", [P, 2, LT])
        nmx = sb("nmx", [P, 2, LT])
        spare = sb("spare", [P, LT + 1])
        total = sb("total", [P, 2, LT])
        share = sb("share", [P, 3, LT])
        stat = sb("stat", [P, LT, 6])
        mv = sb("mv", [P, LT, 2])
        std = sb("std", [P, LT])

        psS = ps("psS", [P, 4, L])
        psT = ps("psT", [P, 2, L])
        psO = ps("psO", [P, 2, L])

        loaded = sem("loaded")
        ctx_loaded = sem("ctx_loaded")
        res_loaded = sem("res_loaded")
        mask_loaded = sem("mask_loaded")
        bias_ready = sem("bias_ready")
        proj_full = sem("proj_full")
        proj_act = sem("proj_act")
        proj_dve = sem("proj_dve")
        s_full = sem("s_full")
        s_read = sem("s_read")
        max_ready = sem("max_ready")
        p_ready = sem("p_ready")
        t_full = sem("t_full")
        t_act = sem("t_act")
        t_dve = sem("t_dve")
        av_full = sem("av_full")
        share_ready = sem("share_ready")
        o_ready = sem("o_ready")
        out_full = sem("out_full")
        step = sem("step")
        var_ready = sem("var_ready")
        std_ready = sem("std_ready")
        added = sem("added")
        res_ready = sem("res_ready")
        NPROJ = 3 * NM
        LOADS = 6
        MASKED = -1e30
        STEPS = 15
        ROOT_AT = 1
        TURNS = NH * LT + NM

        def sequences(eng, body):
            body(0, True)
            with eng.Fori(1, NB) as b:
                body(b, False)

        with nc.Block() as block:
            @block.sync
            def _(sp):
                for dst, name in ((wk, "wk"), (wv, "wv"), (wq, "wq"), (ident, "ident"), (wo, "wo")):
                    sp.dma_start(dst[:], d[name]).then_inc(loaded, 16)
                sp.dma_start(rows[:], d["rows"].partition_broadcast(P)).then_inc(loaded, 16)
                with sp.Fori(0, NB) as b:
                    sp.wait_ge(proj_full, NPROJ * b + 1)
                    sp.dma_start(ctxT[:], d["ctxT"][:, :, bass.ts(b, L)]).then_inc(ctx_loaded, 16)
                    sp.wait_ge(added, b + 1)
                    sp.dma_start(res[:], d["ctx"].rearrange("(b t p) c -> b p t c", p=P, t=LT)[b]).then_inc(res_loaded, 16)

            @block.gpsimd
            def _(pool):
                pool.wait_ge(loaded, 16 * LOADS)
                with pool.Fori(0, NB) as b:
                    pool.wait_ge(s_read, b * NH * LT + LT)
                    pool.dma_start(mask[:], d["mask"].rearrange("b (t p) k -> b p t k", p=P)[b]).then_inc(mask_loaded, 16)
                    pool.wait_ge(res_loaded, 16 * b + 16)
                    pool.tensor_tensor(res[:], res[:], rows[:, 0:1, :].broadcast_to([P, LT, D]), ALU.add)\
                        .then_inc(res_ready, 1)

            @block.tensor
            def _(pe):
                pe.nop().then_inc(proj_full, 1)
                pe.wait_ge(loaded, 16 * LOADS)

                def project(b):
                    pe.wait_ge(ctx_loaded, 16 * b + 16)
                    pe.wait_ge(s_read, b * NH * LT + LT)
                    for n in range(NPROJ):
                        sem_, half = (proj_act, proj_dve)[n % 2], n // 2
                        pe.wait_ge(sem_, b * NPROJ // 2 + half + 1)
                        what, m = divmod(n, NM)
                        for k in range(KD):
                            if what == 0:
                                w, r = wk[:, k, m * P:(m + 1) * P], ctxT[:, k, :]
                            elif what == 1:
                                w, r = ctxT[:, k, m // 2 * P:(m // 2 + 1) * P], wv[:, k, m % 2 * L:(m % 2 + 1) * L]
                            else:
                                w, r = wq[:, k, m * P:(m + 1) * P], xT[:, k, bass.ts(b, L)]
                            mm = pe.matmul(psS[:, n % 4, :], w, r, start=(k == 0), stop=(k == KD - 1))
                        mm.then_inc(proj_full, 1)
                    pe.wait_ge(proj_act, (b + 1) * (NPROJ // 2) + 2)
                    pe.wait_ge(proj_dve, (b + 1) * (NPROJ // 2) + 2)

                def scores(b, h, t):
                    at = HD * (h % 2)
                    pe.wait_ge(s_read, (b * NH + h) * LT + t + 1)
                    pe.matmul(psS[:, t, :], qT[at:at + HD, h // 2, t * P:(t + 1) * P], kT[at:at + HD, h // 2, :],
                              start=True, stop=True).then_inc(s_full, 1)

                def turn(b, n, src):
                    pe.wait_ge((t_act, t_dve)[n % 2], b * (TURNS // 2) + n // 2 + 1)
                    for t in range(LT):
                        mm = pe.transpose(psT[:, n % 2, t * P:(t + 1) * P], src(t), ident[:])
                    mm.then_inc(t_full, 1)

                def attend(b, h, t):
                    if t == 0:
                        pe.wait_ge(o_ready, b * NH + h + 1)
                        pe.wait_ge(t_act, b * (TURNS // 2) + (h + 1) * LT // 2 + 1)
                        pe.wait_ge(t_dve, b * (TURNS // 2) + (h + 1) * LT // 2 + 1)
                    for k in range(LT):
                        mm = pe.matmul(psO[:, h % 2, t * HD:(t + 1) * HD], pT[:, h % 2, k, t * P:(t + 1) * P],
                                       v[:, k, h * HD:(h + 1) * HD], start=(k == 0), stop=(k == LT - 1))
                    if t == LT - 1:
                        mm.then_inc(av_full, 1)

                def sequence(b, first):
                    project(b)
                    for h in range(2):
                        for t in range(LT):
                            scores(b, h, t)
                    for h in range(NH):
                        for t in range(LT):
                            pe.wait_ge(p_ready, (b * NH + h) * LT + t + 1)
                            turn(b, h * LT + t, lambda k: pr[:, h % 3, t, k * P:(k + 1) * P])
                            if h + 2 < NH:
                                scores(b, h + 2, t)
                            if h >= 1:
                                attend(b, h - 1, t)
                    for t in range(LT):
                        attend(b, NH - 1, t)
                    for m in range(NM):
                        pe.wait_ge(o_ready, b * NH + 2 * m + 4)
                        turn(b, NH * LT + m, lambda t: o[:, t, m * P:(m + 1) * P])
                    pe.wait_ge(t_act, (b + 1) * (TURNS // 2) + 1)
                    pe.wait_ge(t_dve, (b + 1) * (TURNS // 2) + 1)
                    for t in range(LT):
                        for m in range(NM):
                            mm = pe.matmul(psO[:, t // 2, t % 2 * D:(t % 2 + 1) * D], oT[:, m, t * P:(t + 1) * P],
                                           wo[:, m, :], start=(m == 0), stop=(m == NM - 1))
                    mm.then_inc(out_full, 1)

                sequences(pe, sequence)

            def copy_proj(eng, copy, done, b, odd):
                for n in range(odd, NPROJ, 2):
                    eng.wait_ge(proj_full, b * NPROJ + n + 1 + 1)
                    what, m = divmod(n, NM)
                    dst = (kT[:, m, :], v[:, m // 2, m % 2 * L:(m % 2 + 1) * L], qT[:, m, :])[what]
                    copy(dst, psS[:, n % 4, :], HD ** -0.5 if what == 2 else 1.0).then_inc(done, 1)

            def copy_turned(eng, copy, done, b, n):
                eng.wait_ge(t_full, b * TURNS + n + 1)
                h = n // LT
                if 2 <= h < NH:
                    eng.wait_ge(av_full, b * NH + h - 1)
                if h < NH:
                    t = n % LT
                    copy(pT[:, h % 2, :, t * P:(t + 1) * P], psT[:, n % 2, :].rearrange("p (k q) -> p k q", q=P), 1.0)\
                        .then_inc(done, 1)
                else:
                    copy(oT[:, n - NH * LT, :], psT[:, n % 2, :], 1.0).then_inc(done, 1)

            @block.scalar
            def _(act):
                act.nop().then_inc(proj_act, 2)
                act.nop().then_inc(t_act, 1)
                copy = lambda dst, src, scale: act.activation(dst, src, ACT.Copy, scale=scale)

                def softmax(b, h, t):
                    if t == 0:
                        act.wait_ge(max_ready, b * NH + h + 1)
                    s = pr[:, h % 3, t, :]
                    act.activation(s, s, ACT.Exp, bias=nmx[:, h % 2, t:t + 1],
                                   accum_out=total[:, h % 2, t:t + 1]).then_inc(p_ready, 1)

                def root(b):
                    act.wait_ge(var_ready, b + 1)
                    act.activation(std[:], mv[:, :, 1], ACT.Sqrt, scale=D / (D - 1)).then_inc(std_ready, 1)

                def sequence(b, first):
                    copy_proj(act, copy, proj_act, b, 0)
                    for t in range(LT):
                        softmax(b, 0, t)
                    for h in range(NH):
                        for t in range(LT):
                            if t % 2 == 0:
                                copy_turned(act, copy, t_act, b, h * LT + t)
                            if h + 1 < NH:
                                softmax(b, h + 1, t)
                        if h == ROOT_AT and not first:
                            root(b - 1)
                    for m in range(0, NM, 2):
                        copy_turned(act, copy, t_act, b, NH * LT + m)

                sequences(act, sequence)
                root(NB - 1)

            @block.vector
            def _(dve):
                dve.nop().then_inc(proj_dve, 2)
                dve.nop().then_inc(t_dve, 1)
                dve.nop().then_inc(s_read, LT)
                dve.nop().then_inc(o_ready, 2)
                dve.nop().then_inc(added, 1)
                dve.wait_ge(loaded, 16 * LOADS)
                copy = lambda dst, src, scale: dve.tensor_scalar(dst, src, scale, None, ALU.mult)

                def row_max(b, h, t):
                    n = b * NH + h
                    if h == 0 and t == 0:
                        dve.wait_ge(bias_ready, b + 1)
                    if h >= 3 and t == 0:
                        dve.wait_ge(t_full, b * TURNS + (h - 2) * LT)
                    dve.wait_ge(s_full, n * LT + t + 1)
                    dve.memset(spare[:, t:t + 1], 0.0)
                    dve.tensor_tensor_reduce(pr[:, h % 3, t, :], psS[:, t, :], bias[:, t, :], 1.0, -3e38,
                                             ALU.add, ALU.max, mx[:, h % 2, t:t + 1]).then_inc(s_read, 1)
                    if t == LT - 1:
                        dve.wait_ge(s_read, (n + 1) * LT + LT)
                        dve.tensor_scalar(nmx[:, h % 2, :], mx[:, h % 2, :], -1.0, None, ALU.mult).then_inc(max_ready, 1)

                def invert(b, h):
                    dve.wait_ge(p_ready, (b * NH + h + 1) * LT)
                    dve.wait_ge(o_ready, b * NH + max(h, 2))
                    dve.reciprocal(share[:, h % 3, :], total[:, h % 2, :]).then_inc(share_ready, 1)

                def scale_out(b, h):
                    n = b * NH + h
                    dve.wait_ge(share_ready, n + 1)
                    dve.wait_ge(av_full, n + 1)
                    dve.tensor_tensor(o[:, :, h * HD:(h + 1) * HD],
                                      psO[:, h % 2, 0:LT * HD].rearrange("p (t e) -> p t e", t=LT),
                                      share[:, h % 3, :].unsqueeze(2).broadcast_to([P, LT, HD]), ALU.mult).then_inc(o_ready, 1)

                steps = [0]

                def link(b, ins):
                    steps[0] = steps[0] % STEPS + 1
                    ins.then_inc(step, 1)
                    dve.wait_ge(step, STEPS * b + steps[0])

                def add_out(b):
                    dve.wait_ge(out_full, b + 1)
                    dve.wait_ge(res_ready, b + 1)
                    for g in range(2):
                        link(b, dve.tensor_tensor(res[:, 2 * g:2 * g + 2, :], res[:, 2 * g:2 * g + 2, :],
                                                  psO[:, g, :].rearrange("p (t c) -> p t c", t=2), ALU.add))

                def statistics(b):
                    for t in range(LT):
                        link(b, dve.bn_stats(stat[:, t, :], res[:, t, :]))
                    dve.memset(spare[:, LT:LT + 1], 0.0)
                    for t in range(LT):
                        ins = dve.bn_aggr(mv[:, t, :], stat[:, t, :])
                    ins.then_inc(var_ready, 1)

                def normalise(b):
                    dve.wait_ge(std_ready, b + 1)
                    link(b, dve.tensor_scalar(std[:], std[:], 1e-3, None, ALU.add))
                    link(b, dve.reciprocal(std[:], std[:]))
                    for t in range(LT):
                        link(b, dve.tensor_scalar(res[:, t, :], res[:, t, :], mv[:, t, 0:1], std[:, t:t + 1],
                                                  ALU.subtract, ALU.mult))

                def scale(b):
                    link(b, dve.tensor_tensor(res[:], res[:], rows[:, 1:2, :].broadcast_to([P, LT, D]), ALU.mult))

                def shift(b):
                    link(b, dve.tensor_tensor(res[:], res[:], rows[:, 2:3, :].broadcast_to([P, LT, D]), ALU.add))

                def add_to_x(b):
                    xs = x[:, bass.ts(b, LT), :]
                    link(b, dve.tensor_tensor(xs, xs, res[:], ALU.add))
                    dve.nop().then_inc(added, 1)

                norm_parts = {ROOT_AT: statistics, ROOT_AT + 1: normalise, ROOT_AT + 2: scale,
                              ROOT_AT + 3: shift, ROOT_AT + 4: add_to_x}

                def sequence(b, first):
                    dve.wait_ge(mask_loaded, 16 * b + 16)
                    dve.tensor_scalar(bias[:], mask[:], MASKED, None, ALU.mult).then_inc(bias_ready, 1)
                    copy_proj(dve, copy, proj_dve, b, 1)
                    for h in range(2):
                        for t in range(LT):
                            row_max(b, h, t)
                    for h in range(NH):
                        if h >= 2:
                            scale_out(b, h - 2)
                        invert(b, h)
                        for t in range(LT):
                            if t % 2 == 1:
                                copy_turned(dve, copy, t_dve, b, h * LT + t)
                            if h + 2 < NH:
                                row_max(b, h + 2, t)
                        if h in norm_parts and not first:
                            norm_parts[h](b - 1)
                    scale_out(b, NH - 2)
                    scale_out(b, NH - 1)
                    for m in range(1, NM, 2):
                        copy_turned(dve, copy, t_dve, b, NH * LT + m)
                    add_out(b)

                sequences(dve, sequence)
                for part in norm_parts.values():
                    part(NB - 1)


def moe_stage(nc, d, x, xT):
    NE, F = 9, 1024
    NR = NE - 1
    NF = F // P
    OFFSET = 2 * NB + 1
    with ExitStack() as ctx:
        sb = lambda name, shape, dt=F32: ctx.enter_context(nc.sbuf_tensor("e_" + name, shape, dt))
        ps = lambda name, shape: ctx.enter_context(nc.psum_tensor("e_" + name, shape, F32))
        sem = lambda name: nc.alloc_semaphore("e_" + name)

        rw = sb("rw", [P, KD, NR])
        index = sb("index", [P, NR])
        prob = sb("prob", [P, NT, NR])
        left = sb("left", [P, NT, NR])
        hit = sb("hit", [P, NT, NR])
        best = sb("best", [P, NT])
        gate = sb("gate", [P, NT, NE])
        up = sb("up", [P, 2, KD, F])
        down = sb("down", [P, 2, NF, D])
        h = sb("h", [P, 2, NF, L])
        psU = ps("psU", [P, 4, L])
        psD = ps("psD", [P, 2, LT, D])

        loaded = sem("loaded")
        up_loaded = [sem(f"up_loaded{s}") for s in range(2)]
        down_loaded = [sem(f"down_loaded{s}") for s in range(2)]
        logits = sem("logits")
        step = sem("step")
        centred = sem("centred")
        exped = sem("exped")
        gates_ready = sem("gates_ready")
        up_full = sem("up_full")
        h_ready = sem("h_ready")
        down_full = sem("down_full")
        added = sem("added")

        def experts(eng, body):
            with eng.Fori(0, NE // 2) as pair:
                body(2 * pair, 0)
                body(2 * pair + 1, 1)
            body(NE - 1, 0)

        with nc.Block() as block:
            @block.sync
            def _(sp):
                sp.dma_start(rw[:], d["rw"]).then_inc(loaded, 16)
                sp.dma_start(index[:], d["index"].partition_broadcast(P)).then_inc(loaded, 16)

                def load(e, s):
                    sp.wait_ge(down_full, NB * (e - 1) + OFFSET)
                    sp.dma_start(up[:, s], d["up"][e]).then_inc(up_loaded[s], 16)
                    sp.dma_start(down[:, s], d["down"][e]).then_inc(down_loaded[s], 16)

                experts(sp, load)

            @block.tensor
            def _(pe):
                pe.nop().then_inc(down_full, OFFSET)
                pe.wait_ge(loaded, 32)
                for t in range(NT):
                    for k in range(KD):
                        mm = pe.matmul(psU[:, 0, t * NR:(t + 1) * NR], xT[:, k, t * P:(t + 1) * P], rw[:, k, :],
                                       start=(k == 0), stop=(k == KD - 1))
                mm.then_inc(logits, 1)
                pe.wait_ge(centred, 1)

                def lift(e, s, b):
                    if b == 0:
                        pe.wait_ge(up_loaded[s], 8 * (e - s) + 16)
                    for m in range(NF):
                        pe.wait_ge(h_ready, (e * NB + b) * NF + m + 1)
                        for k in range(KD):
                            mm = pe.matmul(psU[:, m % 4, :], up[:, s, k, m * P:(m + 1) * P],
                                           xT[:, k, b * L:(b + 1) * L], start=(k == 0), stop=(k == KD - 1))
                        mm.then_inc(up_full, 1)

                def lower(e, s, b):
                    if b == 0:
                        pe.wait_ge(down_loaded[s], 8 * (e - s) + 16)
                    pe.wait_ge(h_ready, (e * NB + b + 1) * NF + 4)
                    pe.wait_ge(added, (e * NB + b + 1) * LT)
                    for t in range(LT):
                        for m in range(NF):
                            mm = pe.matmul(psD[:, b % 2, t, :], h[:, b % 2, m, t * P:(t + 1) * P], down[:, s, m, :],
                                           start=(m == 0), stop=(m == NF - 1))
                    mm.then_inc(down_full, 1)

                def body(e, s):
                    for b in range(NB):
                        lift(e, s, b)
                        if b >= 1:
                            lower(e, s, b - 1)
                    lower(e, s, NB - 1)

                experts(pe, body)

            @block.scalar
            def _(act):
                act.nop().then_inc(h_ready, 4)
                act.wait_ge(centred, 1)
                act.activation(prob[:], prob[:], ACT.Exp).then_inc(exped, 1)

                def body(e, s):
                    for b in range(NB):
                        act.wait_ge(down_full, e * NB + b - 1 + OFFSET)
                        for m in range(NF):
                            act.wait_ge(up_full, (e * NB + b) * NF + m + 1)
                            act.activation(h[:, b % 2, m, :], psU[:, m % 4, :], ACT.Gelu).then_inc(h_ready, 1)

                experts(act, body)

            @block.vector
            def _(dve):
                dve.nop().then_inc(added, 2 * LT)
                steps = [0]

                def link(ins):
                    steps[0] += 1
                    ins.then_inc(step, 1)
                    dve.wait_ge(step, steps[0])

                spread = lambda a: a[:].unsqueeze(2).broadcast_to([P, NT, NR])
                over = lambda a: a[:].unsqueeze(1).broadcast_to([P, NT, NR])
                dve.wait_ge(loaded, 32)
                dve.wait_ge(logits, 1)
                lg = psU[:, 0, 0:NT * NR].rearrange("p (t e) -> p t e", t=NT)
                link(dve.tensor_reduce(best[:], lg, AX_X, ALU.max))
                dve.tensor_tensor(prob[:], lg, spread(best), ALU.subtract).then_inc(centred, 1)
                dve.wait_ge(exped, 1)
                link(dve.tensor_reduce(best[:], prob[:], AX_X, ALU.add))
                link(dve.reciprocal(best[:], best[:]))
                link(dve.tensor_tensor(prob[:], prob[:], spread(best), ALU.mult))
                link(dve.tensor_copy(left[:], prob[:]))
                link(dve.memset(gate[:], 1.0))
                for r in range(2):
                    link(dve.tensor_reduce(best[:], left[:], AX_X, ALU.max))
                    link(dve.tensor_tensor(hit[:], left[:], spread(best), ALU.is_equal))
                    link(dve.tensor_tensor(hit[:], hit[:], over(index), ALU.mult))
                    link(dve.tensor_reduce(best[:], hit[:], AX_X, ALU.min))
                    link(dve.tensor_tensor(hit[:], over(index), spread(best), ALU.is_equal))
                    link(dve.scalar_tensor_tensor(left[:], hit[:], -3.0, left[:], ALU.mult, ALU.add))
                link(dve.tensor_scalar(hit[:], left[:], 0.0, None, ALU.is_lt))
                link(dve.tensor_tensor(gate[:, :, 1:NE], prob[:], hit[:], ALU.mult))
                link(dve.tensor_scalar(x[:], x[:], 2.0, None, ALU.mult))

                def body(e, s):
                    for b in range(NB):
                        dve.wait_ge(down_full, e * NB + b + 1 + OFFSET)
                        for t in range(LT):
                            xs = x[:, LT * b + t, :]
                            dve.scalar_tensor_tensor(xs, psD[:, b % 2, t, :], gate[:, LT * b + t, bass.ds(e, 1)], xs,
                                                     ALU.mult, ALU.add).then_inc(added, 1)

                experts(dve, body)


def causal_attention_stage(nc, d, x, xT):
    NH, HD, RANK = 16, 16, 32
    HT = P // RANK
    NM = NH // HT
    HB = NH // 2
    with ExitStack() as ctx:
        sb = lambda name, shape, dt=F32: ctx.enter_context(nc.sbuf_tensor("a_" + name, shape, dt))
        ps = lambda name, shape: ctx.enter_context(nc.psum_tensor("a_" + name, shape, F32))
        sem = lambda name: nc.alloc_semaphore("a_" + name)

        ident = sb("ident", [P, P])
        w = {n: sb(n, [P, KD, D]) for n in ("aq", "ak", "av", "ao")}
        lsr = {n: sb(n, [P, KD, 2 * P]) for n in ("lq", "lk")}
        cols = sb("cols", [P, 2, KD])
        rows = sb("rows", [P, 2, D])
        tri = sb("tri", [P, L])
        xb = sb("xb", [P, KD, L])
        qk = sb("qk", [P, 2, KD, L])
        qkl = sb("qkl", [P, 2, NM, L])
        v = sb("v", [P, LT, D])
        pr = sb("pr", [P, 3, LT, L])
        pT = sb("pT", [P, 2, LT, L])
        o = sb("o", [P, LT, D])
        oT = sb("oT", [P, KD, L])
        mx = sb("mx", [P, 2, LT])
        nmx = sb("nmx", [P, 2, LT])
        spare = sb("spare", [P, LT + 1])
        total = sb("total", [P, 2, HB, LT])
        share = sb("share", [P, 2, HB, LT])

        psS = ps("psS", [P, 4, L])
        psT = ps("psT", [P, 2, L])
        psO = ps("psO", [P, 2, L])

        loaded = sem("loaded")
        xb_ready = sem("xb_ready")
        proj_full = sem("proj_full")
        proj_act = sem("proj_act")
        proj_dve = sem("proj_dve")
        s_full = sem("s_full")
        s_read = sem("s_read")
        max_ready = sem("max_ready")
        p_ready = sem("p_ready")
        t_full = sem("t_full")
        t_act = sem("t_act")
        t_dve = sem("t_dve")
        av_full = sem("av_full")
        share_ready = sem("share_ready")
        o_ready = sem("o_ready")
        out_full = sem("out_full")
        out_step = sem("out_step")
        LOADS = 10
        TURNS = NH * LT + KD
        PROJ = [("qk", 0, 0), ("qk", 1, 1), ("qk", 2, 0), ("qk", 3, 1)]
        PROJ += [("qkl", m, m % 2) for m in range(2 * NM)] + [("v", 0, 1), ("v", 1, 1)]
        NPROJ = len(PROJ)
        BY = [sum(p[2] == e for p in PROJ) for e in range(2)]
        RANKOF = [sum(p[2] == PROJ[n][2] for p in PROJ[:n]) for n in range(NPROJ)]

        with nc.Block() as block:
            @block.sync
            def _(sp):
                for dst, name in ((w["aq"], "aq"), (w["ak"], "ak"), (w["av"], "av"), (lsr["lq"], "lq"), (lsr["lk"], "lk"),
                                  (cols, "acols"), (tri, "tri"), (ident, "ident"), (w["ao"], "ao")):
                    sp.dma_start(dst[:], d[name]).then_inc(loaded, 16)
                sp.dma_start(rows[:], d["arows"].partition_broadcast(P)).then_inc(loaded, 16)

            @block.gpsimd
            def _(pool):
                with pool.Fori(0, NB) as b:
                    pool.wait_ge(proj_full, NPROJ * b + 1)
                    pool.tensor_copy(xb[:], xT[:, :, bass.ts(b, L)]).then_inc(xb_ready, 1)

            @block.tensor
            def _(pe):
                pe.nop().then_inc(proj_full, 1)
                pe.wait_ge(loaded, 16 * LOADS)

                def project(b):
                    pe.wait_ge(xb_ready, b + 1)
                    pe.wait_ge(s_read, b * NH * LT + LT)
                    for n, (what, m, _) in enumerate(PROJ):
                        if n >= 4:
                            e = PROJ[n - 4][2]
                            pe.wait_ge((proj_act, proj_dve)[e], b * BY[e] + RANKOF[n - 4] + 1)
                        out = psS[:, n % 4, :]
                        if what == "qk":
                            a, t = divmod(m, KD)
                            for k in range(KD):
                                mm = pe.matmul(out, w[("aq", "ak")[a]][:, k, t * P:(t + 1) * P], xb[:, k, :],
                                               start=(k == 0), stop=(k == KD - 1))
                        elif what == "qkl":
                            a, t = divmod(m, NM)
                            src = a * KD + t // 2
                            e = PROJ[src][2]
                            pe.wait_ge((proj_act, proj_dve)[e], b * BY[e] + RANKOF[src] + 1)
                            mm = pe.matmul(out, lsr[("lq", "lk")[a]][:, t // 2, t % 2 * P:(t % 2 + 1) * P],
                                           qk[:, a, t // 2, :], start=True, stop=True)
                        else:
                            for t in range(2):
                                for k in range(KD):
                                    mm = pe.matmul(out[:, t * D:(t + 1) * D], xb[:, k, (2 * m + t) * P:(2 * m + t + 1) * P],
                                                   w["av"][:, k, :], start=(k == 0), stop=(k == KD - 1))
                        mm.then_inc(proj_full, 1)
                    pe.wait_ge(proj_act, (b + 1) * BY[0])
                    pe.wait_ge(proj_dve, (b + 1) * BY[1])

                def scores(b, h, t):
                    at, m, n = RANK * (h % HT), h // HT, (t + 1) * P
                    pe.wait_ge(s_read, (b * NH + h) * LT + t + 1)
                    pe.matmul(psS[:, t, 0:n], qkl[at:at + RANK, 0, m, t * P:n], qkl[at:at + RANK, 1, m, 0:n],
                              start=True, stop=True).then_inc(s_full, 1)

                def turn(b, n, count, src):
                    pe.wait_ge((t_act, t_dve)[n % 2], b * (TURNS // 2) + n // 2 + 1)
                    for i in range(count):
                        mm = pe.transpose(psT[:, n % 2, i * P:(i + 1) * P], src(i), ident[:])
                    mm.then_inc(t_full, 1)

                def attend(b, h, t):
                    if t == 0:
                        if h % HB == 0:
                            pe.wait_ge(o_ready, 4 * b + h // HB + 1)
                        pe.wait_ge(t_act, b * (TURNS // 2) + (h + 1) * LT // 2 + 1)
                        pe.wait_ge(t_dve, b * (TURNS // 2) + (h + 1) * LT // 2 + 1)
                    at = (h % HB * LT + t) * HD
                    for k in range(t + 1):
                        mm = pe.matmul(psO[:, h // HB, at:at + HD], pT[:, h % 2, k, t * P:(t + 1) * P],
                                       v[:, k, h * HD:(h + 1) * HD], start=(k == 0), stop=(k == t))
                    if t == LT - 1:
                        mm.then_inc(av_full, 1)

                with pe.Fori(0, NB) as b:
                    project(b)
                    for h in range(2):
                        for t in range(LT):
                            scores(b, h, t)
                    for h in range(NH):
                        for t in range(LT):
                            pe.wait_ge(p_ready, (b * NH + h) * LT + t + 1)
                            turn(b, h * LT + t, t + 1, lambda k: pr[:, h % 3, t, k * P:(k + 1) * P])
                            if h + 2 < NH:
                                scores(b, h + 2, t)
                            if h >= 1:
                                attend(b, h - 1, t)
                    for t in range(LT):
                        attend(b, NH - 1, t)
                    pe.wait_ge(o_ready, 4 * b + 2 + 2)
                    for m in range(KD):
                        turn(b, NH * LT + m, LT, lambda t: o[:, t, m * P:(m + 1) * P])
                    pe.wait_ge(t_act, (b + 1) * (TURNS // 2) + 1)
                    pe.wait_ge(t_dve, (b + 1) * (TURNS // 2) + 1)
                    for t in range(LT):
                        for m in range(KD):
                            mm = pe.matmul(psO[:, t // 2, t % 2 * D:(t % 2 + 1) * D], oT[:, m, t * P:(t + 1) * P],
                                           w["ao"][:, m, :], start=(m == 0), stop=(m == KD - 1))
                    mm.then_inc(out_full, 1)

            def copy_proj(eng, affine, done, b, who):
                for n, (what, m, e) in enumerate(PROJ):
                    if e != who:
                        continue
                    eng.wait_ge(proj_full, b * NPROJ + n + 1 + 1)
                    src = psS[:, n % 4, :]
                    if what == "qk":
                        a, t = divmod(m, KD)
                        affine(qk[:, a, t, :], src, 1.0, cols[:, a, t:t + 1]).then_inc(done, 1)
                    elif what == "qkl":
                        a, t = divmod(m, NM)
                        affine(qkl[:, a, t, :], src, RANK ** -0.5 if a == 0 else 1.0, 0.0).then_inc(done, 1)
                    else:
                        eng.tensor_tensor(v[:, 2 * m:2 * m + 2, :], src.rearrange("p (t c) -> p t c", t=2),
                                          rows[:, 0:1, :].broadcast_to([P, 2, D]), ALU.add).then_inc(done, 1)

            def copy_turned(eng, copy, done, b, n):
                eng.wait_ge(t_full, b * TURNS + n + 1)
                h = n // LT
                if 2 <= h < NH:
                    eng.wait_ge(av_full, b * NH + h - 1)
                if h < NH:
                    t = n % LT
                    copy(pT[:, h % 2, 0:t + 1, t * P:(t + 1) * P],
                         psT[:, n % 2, 0:(t + 1) * P].rearrange("p (k q) -> p k q", q=P)).then_inc(done, 1)
                else:
                    copy(oT[:, n - NH * LT, :], psT[:, n % 2, :]).then_inc(done, 1)

            @block.scalar
            def _(act):
                act.nop().then_inc(t_act, 1)
                act.wait_ge(loaded, 16 * LOADS)
                affine = lambda dst, src, scale, bias: act.activation(dst, src, ACT.Identity, scale=scale, bias=bias)
                copy = lambda dst, src: act.copy(dst, src)

                def softmax(b, h, t):
                    if t == 0:
                        act.wait_ge(max_ready, b * NH + h + 1)
                    s = pr[:, h % 3, t, 0:(t + 1) * P]
                    act.activation(s, s, ACT.Exp, bias=nmx[:, h % 2, t:t + 1],
                                   accum_out=total[:, h // HB, h % HB, t:t + 1]).then_inc(p_ready, 1)

                with act.Fori(0, NB) as b:
                    copy_proj(act, affine, proj_act, b, 0)
                    for t in range(LT):
                        softmax(b, 0, t)
                    for h in range(NH):
                        for t in range(LT):
                            if t % 2 == 0:
                                copy_turned(act, copy, t_act, b, h * LT + t)
                            if h + 1 < NH:
                                softmax(b, h + 1, t)
                    copy_turned(act, copy, t_act, b, NH * LT)

            @block.vector
            def _(dve):
                dve.nop().then_inc(t_dve, 1)
                dve.nop().then_inc(s_read, LT)
                dve.nop().then_inc(o_ready, 2)
                dve.wait_ge(loaded, 16 * LOADS)
                affine = lambda dst, src, scale, bias: dve.tensor_scalar(dst, src, scale, bias, ALU.mult, ALU.add)
                copy = lambda dst, src: dve.tensor_copy(dst, src)

                def row_max(b, h, t):
                    n = b * NH + h
                    if h >= 3 and t == 0:
                        dve.wait_ge(t_full, b * TURNS + (h - 2) * LT)
                    if h >= 2 and t == 0:
                        dve.wait_ge(p_ready, (n - 1) * LT)
                    dve.wait_ge(s_full, n * LT + t + 1)
                    dve.memset(spare[:, t:t + 1], 0.0)
                    e = (t + 1) * P
                    dve.tensor_tensor_reduce(pr[:, h % 3, t, 0:e], psS[:, t, 0:e], tri[:, L - e:L], 1.0, -3e38,
                                             ALU.add, ALU.max, mx[:, h % 2, t:t + 1]).then_inc(s_read, 1)
                    if t == LT - 1:
                        dve.wait_ge(s_read, (n + 1) * LT + LT)
                        dve.tensor_scalar(nmx[:, h % 2, :], mx[:, h % 2, :], -1.0, None, ALU.mult).then_inc(max_ready, 1)

                def scale_out(b, g):
                    dve.wait_ge(p_ready, (b * NH + (g + 1) * HB) * LT)
                    dve.reciprocal(share[:, g], total[:, g]).then_inc(share_ready, 1)
                    dve.wait_ge(share_ready, 2 * b + g + 1)
                    dve.wait_ge(av_full, b * NH + (g + 1) * HB)
                    dve.tensor_tensor(
                        o[:, :, g * HB * HD:(g + 1) * HB * HD].rearrange("p t (h e) -> p h t e", h=HB),
                        psO[:, g, :].rearrange("p (h t e) -> p h t e", h=HB, t=LT),
                        share[:, g].unsqueeze(3).broadcast_to([P, HB, LT, HD]), ALU.mult).then_inc(o_ready, 1)

                with dve.Fori(0, NB) as b:
                    copy_proj(dve, affine, proj_dve, b, 1)
                    for h in range(2):
                        for t in range(LT):
                            row_max(b, h, t)
                    for h in range(NH):
                        for t in range(LT):
                            if t % 2 == 1:
                                copy_turned(dve, copy, t_dve, b, h * LT + t)
                            if h + 2 < NH:
                                row_max(b, h + 2, t)
                        if h == HB + 1:
                            scale_out(b, 0)
                    scale_out(b, 1)
                    copy_turned(dve, copy, t_dve, b, NH * LT + 1)
                    dve.wait_ge(out_full, b + 1)
                    for g in range(2):
                        xs = x[:, bass.ds(4 * b + 2 * g, 2), :]
                        dve.tensor_tensor(xs, xs, psO[:, g, :].rearrange("p (t c) -> p t c", t=2), ALU.add)\
                           .then_inc(o_ready, 1)
                    xs = x[:, bass.ts(b, LT), :]
                    dve.wait_ge(o_ready, 4 * b + 6)
                    dve.tensor_tensor(xs, xs, rows[:, 1:2, :].broadcast_to([P, LT, D]), ALU.add).then_inc(out_step, 1)


def retention_stage(nc, d, x, xT):
    NH, HD, PAD = 16, 16, 32
    HM = P // PAD
    NM = NH // HM
    with ExitStack() as ctx:
        sb = lambda name, shape, dt=F32: ctx.enter_context(nc.sbuf_tensor("r_" + name, shape, dt))
        ps = lambda name, shape: ctx.enter_context(nc.psum_tensor("r_" + name, shape, F32))
        sem = lambda name: nc.alloc_semaphore("r_" + name)

        ident = sb("ident", [P, P])
        w = {n: sb(n, [P, KD, D]) for n in ("rq", "rk", "rv", "rg", "ro")}
        rows = sb("rows", [P, 2, D])
        table = sb("table", [P, 2, 2, LT, D])
        keep = sb("keep", [P, P])
        own = sb("own", [P, HM * HD])
        eps = sb("eps", [P, 1])
        xb = sb("xb", [P, KD, L])
        cb = sb("cb", [P, KD, L])
        v = sb("v", [P, LT, D])
        part = sb("part", [P, 2, 2, 2, D])
        pad = sb("pad", [P, 2, LT, NH, PAD])
        padT = sb("padT", [P, 2, NM, L])
        gate = sb("gate", [P, LT, D])
        state = sb("state", [P, LT - 1, NM, HM * HD])
        sim = sb("sim", [P, 2, LT, P])
        r = sb("r", [P, LT, D])
        sq = sb("sq", [P, LT, D])
        mean = sb("mean", [P, LT * NH])
        var = sb("var", [P, LT * NH])
        rT = sb("rT", [P, KD, L])

        psR = ps("psR", [P, 4, L])
        psS = ps("psS", [P, 2, L])
        psX = ps("psX", [P, 2, L])

        loaded = sem("loaded")
        eps_ready = sem("eps_ready")
        zeroed = sem("zeroed")
        cb_loaded = sem("cb_loaded")
        xb_ready = sem("xb_ready")
        proj_full = sem("proj_full")
        v_ready = sem("v_ready")
        rot_step = sem("rot_step")
        rot_ready = sem("rot_ready")
        g_plus = sem("g_plus")
        g_ready = sem("g_ready")
        t_full = sem("t_full")
        t_copied = sem("t_copied")
        st_full = sem("st_full")
        st_ready = sem("st_ready")
        sim_full = sem("sim_full")
        sim_ready = sem("sim_ready")
        av_done = sem("av_done")
        r_copied = sem("r_copied")
        step = sem("step")
        centred = sem("centred")
        squared = sem("squared")
        var_ready = sem("var_ready")
        std_ready = sem("std_ready")
        r_ready = sem("r_ready")
        out_full = sem("out_full")
        added = sem("added")
        LOADS = 11
        NPROJ = 8
        TURNS = 2 * NM + KD

        with nc.Block() as block:
            @block.sync
            def _(sp):
                for n in ("rv", "rk", "rq", "rg"):
                    sp.dma_start(w[n][:], d[n]).then_inc(loaded, 16)
                sp.dma_start(table[:], d["table"]).then_inc(loaded, 16)
                for dst, n in ((ident, "ident"), (keep, "keep"), (own, "own"), (w["ro"], "ro")):
                    sp.dma_start(dst[:], d[n]).then_inc(loaded, 16)
                sp.dma_start(rows[:], d["rrows"].partition_broadcast(P)).then_inc(loaded, 16)
                sp.nop().then_inc(loaded, 16)
                with sp.Fori(0, NB) as b:
                    sp.wait_ge(proj_full, NPROJ * b + 1)
                    sp.dma_start(cb[:], d["ctxT"][:, :, bass.ts(b, L)]).then_inc(cb_loaded, 16)

            @block.gpsimd
            def _(pool):
                pool.memset(eps[:], 1e-5).then_inc(eps_ready, 1)
                pool.memset(pad[:], 0.0).then_inc(zeroed, 1)
                with pool.Fori(0, NB) as b:
                    pool.wait_ge(proj_full, NPROJ * b + 1)
                    pool.tensor_copy(xb[:], xT[:, :, bass.ts(b, L)]).then_inc(xb_ready, 1)

            @block.tensor
            def _(pe):
                pe.nop().then_inc(proj_full, 1)
                pe.nop().then_inc(av_done, 2)
                pe.wait_ge(loaded, 16 * LOADS)

                def turn(b, n, src):
                    pe.wait_ge(t_copied, b * TURNS + n + 1)
                    for t in range(LT):
                        mm = pe.transpose(psS[:, n % 2, t * P:(t + 1) * P], src(t), ident[:])
                    mm.then_inc(t_full, 1)

                with pe.Fori(0, NB) as b:
                    pe.wait_ge(cb_loaded, 16 * b + 16)
                    pe.wait_ge(xb_ready, b + 1)
                    pe.wait_ge(r_copied, b + 1)
                    for n in range(NPROJ):
                        what, g = divmod(n, 2)
                        if what == 2:
                            pe.wait_ge(v_ready, 2 * b + g + 1)
                        if what == 3:
                            pe.wait_ge(rot_ready, 4 * b + g + 1)
                        src = (cb, cb, xb, xb)[what]
                        for t in range(2):
                            for k in range(KD):
                                mm = pe.matmul(psR[:, n % 4, t * D:(t + 1) * D],
                                               src[:, k, (2 * g + t) * P:(2 * g + t + 1) * P],
                                               w[("rv", "rk", "rq", "rg")[what]][:, k, :],
                                               start=(k == 0), stop=(k == KD - 1))
                        mm.then_inc(proj_full, 1)
                    pe.wait_ge(sim_ready, NH * b + 2)
                    pe.wait_ge(added, 2 * b + 2)
                    for a in range(2):
                        pe.wait_ge(rot_ready, 4 * b + 2 * a + 2)
                        for m in range(NM):
                            turn(b, a * NM + m, lambda t: pad[:, a, t, HM * m:HM * (m + 1), :].rearrange("p h e -> p (h e)"))
                        if a == 0:
                            for c in range(LT - 1):
                                for m in range(NM):
                                    at = c % 2 * D + m * HM * HD
                                    for s in range(c + 1):
                                        mm = pe.matmul(psX[:, c // 2, at:at + HM * HD],
                                                       pad[:, 0, s, HM * m:HM * (m + 1), :].rearrange("p h e -> p (h e)"),
                                                       v[:, s, m * HM * HD:(m + 1) * HM * HD], start=(s == 0), stop=(s == c))
                            mm.then_inc(st_full, 1)
                    pe.wait_ge(t_copied, b * TURNS + 2 * NM + 2)
                    pe.wait_ge(st_ready, 2 * b + 2)
                    pe.wait_ge(g_plus, 2 * b + 2)

                    def similar(h):
                        at, m = PAD * (h % HM), h // HM
                        pe.wait_ge(sim_ready, NH * b + h + 1)
                        for c in range(LT):
                            mm = pe.matmul(psS[:, h % 2, c * P:(c + 1) * P], padT[at:at + PAD, 0, m, c * P:(c + 1) * P],
                                           padT[at:at + PAD, 1, m, c * P:(c + 1) * P], start=True, stop=True)
                        mm.then_inc(sim_full, 1)

                    similar(0)
                    for h in range(NH):
                        m = h // HM
                        if h + 1 < NH:
                            similar(h + 1)
                        if h % HM == 0:
                            for c in range(1, LT):
                                pe.matmul(psR[:, c, m * HM * HD:(m + 1) * HM * HD], padT[:, 1, m, c * P:(c + 1) * P],
                                          state[:, c - 1, m, :], start=True, stop=True)
                        pe.wait_ge(sim_ready, NH * b + h + 1 + 2)
                        for c in range(LT):
                            mm = pe.matmul(psR[:, c, h * HD:(h + 1) * HD], sim[:, h % 2, c, :], v[:, c, h * HD:(h + 1) * HD],
                                           start=(c == 0), stop=True, skip_group_check=True)
                        mm.then_inc(av_done, 1)
                    pe.wait_ge(r_ready, b + 1)
                    for m in range(KD):
                        turn(b, 2 * NM + m, lambda t: r[:, t, m * P:(m + 1) * P])
                    pe.wait_ge(t_copied, (b + 1) * TURNS + 2)
                    for t in range(LT):
                        for m in range(KD):
                            mm = pe.matmul(psX[:, t // 2, t % 2 * D:(t % 2 + 1) * D], rT[:, m, t * P:(t + 1) * P],
                                           w["ro"][:, m, :], start=(m == 0), stop=(m == KD - 1))
                    mm.then_inc(out_full, 1)

            @block.scalar
            def _(act):
                act.nop().then_inc(t_copied, 2)
                act.nop().then_inc(r_copied, 1)
                act.wait_ge(eps_ready, 1)
                with act.Fori(0, NB) as b:
                    act.wait_ge(av_done, NH * b + 2)
                    for g in range(2):
                        act.wait_ge(proj_full, NPROJ * b + g + 1 + 1)
                        act.copy(v[:, 2 * g:2 * g + 2, :], psR[:, g, :].rearrange("p (t c) -> p t c", t=2)).then_inc(v_ready, 1)
                    for n in range(2 * NM):
                        act.wait_ge(t_full, b * TURNS + n + 1)
                        act.copy(padT[:, n // NM, n % NM, :], psS[:, n % 2, :]).then_inc(t_copied, 1)
                    for g in range(2):
                        act.wait_ge(g_plus, 2 * b + g + 1)
                        act.activation(gate[:, 2 * g:2 * g + 2, :], gate[:, 2 * g:2 * g + 2, :], ACT.Silu).then_inc(g_ready, 1)
                    act.wait_ge(av_done, NH * (b + 1) + 2)
                    act.copy(r[:], psR[:, :, 0:D]).then_inc(r_copied, 1)
                    act.wait_ge(centred, b + 1)
                    act.activation(sq[:], r[:], ACT.Square).then_inc(squared, 1)
                    act.wait_ge(var_ready, b + 1)
                    act.activation(var[:], var[:], ACT.Sqrt, scale=1.0 / HD, bias=eps[:]).then_inc(std_ready, 1)
                    for m in range(KD):
                        act.wait_ge(t_full, b * TURNS + 2 * NM + m + 1)
                        act.copy(rT[:, m, :], psS[:, m % 2, :]).then_inc(t_copied, 1)

            @block.vector
            def _(dve):
                dve.nop().then_inc(sim_ready, 2)
                dve.nop().then_inc(added, 2)
                dve.wait_ge(loaded, 16 * LOADS)
                dve.wait_ge(zeroed, 1)
                STEPS = 7
                two = lambda a: a.rearrange("p (t c) -> p t c", t=2)
                with dve.Fori(0, NB) as b:
                    dve.wait_ge(av_done, NH * b + 2)
                    for n in range(4):
                        a, g = divmod(n, 2)
                        dve.wait_ge(proj_full, NPROJ * b + 2 + n + 1 + 1)
                        if n >= 2:
                            dve.wait_ge(rot_ready, 4 * b + n - 1)
                        src = psR[:, (2 + n) % 4, :]
                        dve.tensor_tensor(part[:, n % 2, 0], two(src), table[:, a, 0, 2 * g:2 * g + 2, :], ALU.mult).then_inc(rot_step, 1)
                        for e in range(2):
                            pair = lambda y, e: y.rearrange("p t (i e) -> p t i e", e=2)[:, :, :, e]
                            dve.tensor_tensor(pair(part[:, n % 2, 1], e), pair(two(src), 1 - e),
                                              pair(table[:, a, 1, 2 * g:2 * g + 2, :], e), ALU.mult).then_inc(rot_step, 1)
                        dve.wait_ge(rot_step, 12 * b + 3 * n + 3)
                        for t in range(2):
                            ins = dve.tensor_tensor(pad[:, a, 2 * g + t, :, 0:HD],
                                                    part[:, n % 2, 0, t, :].rearrange("p (h e) -> p h e", e=HD),
                                                    part[:, n % 2, 1, t, :].rearrange("p (h e) -> p h e", e=HD), ALU.add)
                        ins.then_inc(rot_ready, 1)
                    for g in range(2):
                        dve.wait_ge(proj_full, NPROJ * b + 6 + g + 1 + 1)
                        dve.tensor_tensor(gate[:, 2 * g:2 * g + 2, :], two(psR[:, (6 + g) % 4, :]),
                                          rows[:, 0:1, :].broadcast_to([P, 2, D]), ALU.add).then_inc(g_plus, 1)
                    dve.wait_ge(st_full, b + 1)
                    for g, cs in ((0, 2), (1, 1)):
                        dve.tensor_tensor(state[:, 2 * g:2 * g + cs].rearrange("p c m e -> p (c m) e"),
                                          psX[:, g, 0:cs * D].rearrange("p (c e) -> p c e", e=HM * HD),
                                          own[:].unsqueeze(1).broadcast_to([P, cs * NM, HM * HD]), ALU.mult).then_inc(st_ready, 1)
                    for h in range(NH):
                        dve.wait_ge(sim_full, NH * b + h + 1)
                        dve.wait_ge(av_done, NH * b + h + 1)
                        dve.tensor_tensor(sim[:, h % 2], psS[:, h % 2, :].rearrange("p (c n) -> p c n", c=LT),
                                          keep[:].unsqueeze(1).broadcast_to([P, LT, P]), ALU.mult).then_inc(sim_ready, 1)
                    n = [0]

                    def link(ins):
                        n[0] += 1
                        ins.then_inc(step, 1)
                        dve.wait_ge(step, STEPS * b + n[0])

                    heads = r[:].rearrange("p t (h e) -> p (t h) e", e=HD)
                    spread = lambda y: y[:].unsqueeze(2).broadcast_to([P, LT * NH, HD])
                    dve.wait_ge(r_copied, b + 1 + 1)
                    link(dve.tensor_reduce(mean[:], heads, AX_X, ALU.add))
                    link(dve.tensor_scalar(mean[:], mean[:], 1.0 / HD, None, ALU.mult))
                    dve.tensor_tensor(heads, heads, spread(mean), ALU.subtract).then_inc(centred, 1)
                    dve.wait_ge(squared, b + 1)
                    dve.tensor_reduce(var[:], sq[:].rearrange("p t (h e) -> p (t h) e", e=HD), AX_X, ALU.add).then_inc(var_ready, 1)
                    dve.wait_ge(std_ready, b + 1)
                    link(dve.reciprocal(var[:], var[:]))
                    link(dve.tensor_tensor(heads, heads, spread(var), ALU.mult))
                    dve.wait_ge(g_ready, 2 * b + 2)
                    dve.tensor_tensor(r[:], r[:], gate[:], ALU.mult).then_inc(r_ready, 1)
                    dve.wait_ge(out_full, b + 1)
                    for g in range(2):
                        xs = x[:, bass.ds(4 * b + 2 * g, 2), :]
                        link(dve.tensor_tensor(xs, xs, two(psX[:, g, :]), ALU.add))
                    xs = x[:, bass.ts(b, LT), :]
                    link(dve.tensor_tensor(xs, xs, rows[:, 1:2, :].broadcast_to([P, LT, D]), ALU.add))
                    dve.nop().then_inc(added, 2)
                    assert n[0] == STEPS, n


def hashed_moe_stage(nc, d, x, xT, x_dram, out):
    NC, HS, HR = 8, 512, 256
    NI = TOK // NC
    MS, MR = HS // P, HR // P
    EXPERTS = [((11 * r) % NC, (11 * r + 7919) % NC) for r in range(NC)]
    with ExitStack() as ctx:
        sb = lambda name, shape, dt=F32: ctx.enter_context(nc.sbuf_tensor("h_" + name, shape, dt))
        ps = lambda name, shape: ctx.enter_context(nc.psum_tensor("h_" + name, shape, F32))
        sem = lambda name: nc.alloc_semaphore("h_" + name)

        s1 = sb("s1", [P, KD, HS])
        s3 = sb("s3", [P, KD, HS])
        s2 = sb("s2", [P, MS, D])
        w1 = sb("w1", [P, NC, KD, HR])
        w2 = sb("w2", [P, NC, MR, D])
        cols = sb("cols", [P, 2 * MS + NC * MR])
        rows = sb("rows", [1, 1 + NC, D])
        ones = sb("ones", [1, P])
        eps = sb("eps", [P, 1])
        xr = sb("xr", [P, NC, 2, D])
        act1 = sb("act1", [P, 2, NI])
        hs = sb("hs", [P, 2, MS, NI])
        hr = sb("hr", [P, 2, 2, MR, NI])
        stat = sb("stat", [P, 2 * NC, 6])
        mv = sb("mv", [P, 2 * NC, 2])
        rstd = sb("rstd", [P, 2 * NC])

        psU = ps("psU", [P, 4, 2, NI])
        psD = ps("psD", [P, 4, 2, D])

        w_loaded = [sem(f"w_loaded{n}") for n in range(3)]
        x_stored = sem("x_stored")
        x_loaded = sem("x_loaded")
        filled = sem("filled")
        up_full = sem("up_full")
        silu_ready = sem("silu_ready")
        hs_ready = sem("hs_ready")
        hr_ready = sem("hr_ready")
        down_full = sem("down_full")
        halves = sem("halves")
        summed = sem("summed")
        stats = sem("stats")
        var_ready = sem("var_ready")
        std_ready = sem("std_ready")
        inverted = sem("inverted")
        normed = sem("normed")
        out_stored = sem("out_stored")
        UPS = MS + 2
        by_class = lambda a: a.rearrange("(h p r) c -> p r h c", p=P, r=NC)

        with nc.Block() as block:
            @block.sync
            def _(sp):
                sp.dma_start(x_dram.rearrange("(t p) c -> p t c", p=P), x[:]).then_inc(x_stored, 16)
                for n, pairs in enumerate((((s1, "s1"), (s3, "s3"), (cols, "hcols"), (rows, "hrows")),
                                           ((w1, "w1"),), ((w2, "w2"), (s2, "s2")))):
                    for dst, name in pairs:
                        sp.dma_start(dst[:], d[name]).then_inc(w_loaded[n], 16)
                sp.wait_ge(x_stored, 16)
                for r in range(NC):
                    sp.dma_start(xr[:, r], by_class(x_dram)[:, r]).then_inc(x_loaded, 16)
                for r in range(NC):
                    sp.wait_ge(normed, 2 * r + 2)
                    sp.dma_start(by_class(out)[:, r], xr[:, r]).then_inc(out_stored, 16)
                sp.wait_ge(out_stored, 16 * NC)

            @block.gpsimd
            def _(pool):
                pool.memset(ones[:], 1.0).then_inc(filled, 1)
                pool.memset(eps[:], 1e-5).then_inc(filled, 1)

            def up_bank(r, n):
                return psU[:, (r * UPS + n) % 4]

            @block.tensor
            def _(pe):
                pe.wait_ge(filled, 2)

                def bank_free(n):
                    r, m = divmod(n - 4, UPS)
                    if m < MS:
                        pe.wait_ge(hs_ready, MS * r + m + 1)
                    else:
                        pe.wait_ge(hr_ready, 2 * MR * r + MR * (m - MS + 1))

                def up(r):
                    for n in range(UPS):
                        if r * UPS + n >= 4:
                            bank_free(r * UPS + n)
                        if r == 0 and n == 0:
                            pe.wait_ge(w_loaded[0], 64)
                        if r == 0 and n == MS:
                            pe.wait_ge(w_loaded[1], 16)
                        for g in range(2):
                            for k in range(KD):
                                if n < MS:
                                    w = (s1, s3)[g][:, k, n * P:(n + 1) * P]
                                else:
                                    w = w1[:, EXPERTS[r][n - MS], k, g * P:(g + 1) * P]
                                mm = pe.matmul(up_bank(r, n)[:, g, :], w, xT[:, k, r:TOK:NC],
                                               start=(k == 0), stop=(k == KD - 1))
                        mm.then_inc(up_full, 1)

                def down(r):
                    if r == 0:
                        pe.wait_ge(w_loaded[2], 32)
                    pe.wait_ge(hs_ready, MS * (r + 1))
                    pe.wait_ge(hr_ready, 2 * MR * (r + 1))
                    if r >= 2:
                        pe.wait_ge(summed, 2 * (r - 1))
                    for g in range(2):
                        tok = slice(g * P, (g + 1) * P)
                        bank = psD[:, 2 * (r % 2) + g]
                        for m in range(MS):
                            pe.matmul(bank[:, 0, :], hs[:, r % 2, m, tok], s2[:, m, :], start=(m == 0), stop=False)
                        pe.matmul(bank[:, 0, :], ones[:], rows[:, 0, :], start=False, stop=True)
                        for e in range(2):
                            for m in range(MR):
                                pe.matmul(bank[:, 1, :], hr[:, r % 2, e, m, tok], w2[:, EXPERTS[r][e], m, :],
                                          start=(e == 0 and m == 0), stop=False)
                            mm = pe.matmul(bank[:, 1, :], ones[:], rows[:, 1 + EXPERTS[r][e], :], start=False, stop=(e == 1))
                        mm.then_inc(down_full, 1)

                for r in range(NC):
                    up(r)
                    if r >= 1:
                        down(r - 1)
                down(NC - 1)

            @block.scalar
            def _(act):
                act.wait_ge(w_loaded[0], 64)
                for r in range(NC):
                    for m in range(MS):
                        act.wait_ge(up_full, r * UPS + m + 1)
                        if r * MS + m >= 2:
                            act.wait_ge(hs_ready, r * MS + m - 1)
                        act.activation(act1[:, m % 2, :], up_bank(r, m)[:, 0, :], ACT.Silu, bias=cols[:, m:m + 1])\
                           .then_inc(silu_ready, 1)
                    if r >= 2:
                        act.wait_ge(down_full, 2 * (r - 1))
                    for e in range(2):
                        act.wait_ge(up_full, r * UPS + MS + e + 1)
                        for m in range(MR):
                            at = 2 * MS + EXPERTS[r][e] * MR + m
                            act.activation(hr[:, r % 2, e, m, :], up_bank(r, MS + e)[:, m, :], ACT.Gelu,
                                           bias=cols[:, at:at + 1]).then_inc(hr_ready, 1)
                act.wait_ge(filled, 2)
                act.wait_ge(var_ready, 2 * NC)
                act.activation(rstd[:], mv[:, :, 1], ACT.Sqrt, bias=eps[:]).then_inc(std_ready, 1)

            @block.vector
            def _(dve):
                dve.wait_ge(w_loaded[0], 64)

                def gated(r):
                    if r >= 2:
                        dve.wait_ge(down_full, 2 * (r - 1))
                    for m in range(MS):
                        dve.wait_ge(silu_ready, r * MS + m + 1)
                        dve.scalar_tensor_tensor(hs[:, r % 2, m, :], up_bank(r, m)[:, 1, :], cols[:, MS + m:MS + m + 1],
                                                 act1[:, m % 2, :], ALU.add, ALU.mult).then_inc(hs_ready, 1)

                def add(r):
                    dve.wait_ge(x_loaded, 16 * NC)
                    for g in range(2):
                        dve.wait_ge(down_full, 2 * r + g + 1)
                        bank = psD[:, 2 * (r % 2) + g]
                        dve.scalar_tensor_tensor(xr[:, r, g, :], bank[:, 0, :], 0.5, xr[:, r, g, :], ALU.mult, ALU.add)\
                           .then_inc(halves, 1)
                        dve.wait_ge(halves, 2 * r + g + 1)
                        dve.scalar_tensor_tensor(xr[:, r, g, :], bank[:, 1, :], 0.25, xr[:, r, g, :], ALU.mult, ALU.add)\
                           .then_inc(summed, 1)
                    for g in range(2):
                        dve.wait_ge(summed, 2 * r + g + 1)
                        dve.bn_stats(stat[:, 2 * r + g, :], xr[:, r, g, :]).then_inc(stats, 1)
                    for g in range(2):
                        dve.wait_ge(stats, 2 * r + g + 1)
                        dve.bn_aggr(mv[:, 2 * r + g, :], stat[:, 2 * r + g, :]).then_inc(var_ready, 1)

                for r in range(NC):
                    gated(r)
                    if r >= 1:
                        add(r - 1)
                add(NC - 1)
                dve.wait_ge(std_ready, 1)
                dve.reciprocal(rstd[:], rstd[:]).then_inc(inverted, 1)
                dve.wait_ge(inverted, 1)
                for n in range(2 * NC):
                    dve.tensor_scalar(xr[:, n // 2, n % 2, :], xr[:, n // 2, n % 2, :], mv[:, n, 0:1], rstd[:, n:n + 1],
                                      ALU.subtract, ALU.mult).then_inc(normed, 1)


def decoder_kernel(nc, d, out):
    dram = lambda name, shape: nc.dram_tensor(name, shape, F32, kind="Internal").ap()
    yo_dram = dram("yo_dram", [TOK, D])
    bc_dram = dram("bc_dram", [NB, 2, 2 * NS, L])
    x_dram = dram("x_dram", [TOK, D])
    mamba_stage(nc, d, yo_dram, bc_dram)
    with nc.sbuf_tensor("x_rows", [P, NT, D], F32) as x, nc.sbuf_tensor("x_cols", [P, KD, TOK], F32) as xT:
        norm_stage(nc, "n1", x, xT, d["ident"], first=dict(yo=yo_dram, x=d["x"], gb=d["gb"]))
        cross_attention_stage(nc, d, x, xT)
        norm_stage(nc, "n2", x, xT, d["ident"])
        moe_stage(nc, d, x, xT)
        norm_stage(nc, "n3", x, xT, d["ident"])
        causal_attention_stage(nc, d, x, xT)
        norm_stage(nc, "n4", x, xT, d["ident"])
        retention_stage(nc, d, x, xT)
        norm_stage(nc, "n5", x, xT, d["ident"])
        hashed_moe_stage(nc, d, x, xT, x_dram, out)


def k_tiles(w):
    return np.ascontiguousarray(w.reshape(-1, P, w.shape[-1]).transpose(1, 0, 2))


def channels(v):
    return v.reshape(-1, P, v.shape[-1]).transpose(1, 0, 2)


def transposed(a):
    return k_tiles(np.ascontiguousarray(a.reshape(TOK, D).T))


def by_heads(w):
    return k_tiles(w.transpose(1, 0, 2).reshape(D, -1))


def block_diagonal(w):
    out = np.zeros((P, KD, 2 * P), w.dtype)
    for h in range(w.shape[0]):
        t, i = divmod(h, P // w.shape[1])
        out[i * w.shape[1]:(i + 1) * w.shape[1], t, i * w.shape[2]:(i + 1) * w.shape[2]] = w[h]
    return out


def retention_tables():
    H, hd = 16, 16
    gamma = (1.0 - np.exp(np.linspace(np.log(1 / 32), np.log(1 / 512), H)).astype(np.float32)).astype(np.float64)
    base = (np.arange(0, hd, 2) + 0.4 * hd) / (1.4 * hd)
    pos = np.arange(L, dtype=np.float64)[:, None]
    scale = base[None] ** ((pos - L // 2) / 512.0)
    angle = pos / 10000.0 ** (np.arange(hd // 2) / (hd // 2))[None]
    out = np.zeros((2, 2, L, H, hd))
    for a, s, decay in ((0, 1 / scale, gamma[None] ** -pos), (1, scale, gamma[None] ** pos)):
        out[a, 0] = np.repeat(np.cos(angle) * s, 2, -1)[:, None, :] * decay[:, :, None]
        out[a, 1] = (np.repeat(np.sin(angle) * s, 2, -1) * np.tile([-1, 1], hd // 2))[:, None, :] * decay[:, :, None]
    return np.ascontiguousarray(out.reshape(2, 2, LT, P, D).transpose(3, 0, 1, 2, 4)).astype(np.float32)


def laid_out(i):
    both = lambda f: np.ascontiguousarray(np.stack([f("L0_attn_fwd_"), f("L0_attn_bwd_")], axis=1))
    index = np.arange(P)
    tri = np.zeros((P, L), np.float32)
    tri[:, L - P:] = np.where(index[None] > index[:, None], -1e30, 0.0)
    experts = lambda shared, routed, k: np.ascontiguousarray(
        np.concatenate([i[shared], i[routed]]).reshape(9, k, P, -1).transpose(0, 2, 1, 3))
    rows = lambda *names: np.stack([i[n] for n in names])
    x, c = "L0_xattn_", "L1_"
    return {
        "x": i["x"].reshape(TOK, D), "xT": transposed(i["x"]),
        "in_w": both(lambda p: k_tiles(i[p + "in_proj_w"].T)), "xp_w": both(lambda p: k_tiles(i[p + "x_proj_w"].T)),
        "dt_w": both(lambda p: i[p + "dt_proj_w"].T), "out_w": both(lambda p: k_tiles(i[p + "out_proj_w"].T)),
        "small": both(lambda p: channels(np.concatenate(
            [i[p + "conv_w"], i[p + "conv_b"][:, None], i[p + "dt_proj_b"][:, None], i[p + "D"][:, None]], 1))),
        "a_log": both(lambda p: channels(i[p + "A_log"])), "gb": rows("L0_attn_ln_gamma", "L0_attn_ln_beta"),
        "ctx": i["ctx_1024"].reshape(TOK, D), "ctxT": transposed(i["ctx_1024"]), "mask": i["mask_BxSxS2_bk1"],
        "wq": by_heads(i[x + "w_q"]), "wk": by_heads(i[x + "w_k"]), "wv": by_heads(i[x + "w_v"]),
        "wo": k_tiles(i[x + "w_o"]), "rows": rows(x + "b_o", x + "gamma", x + "beta"),
        "rw": k_tiles(i["L0_ffn_router_w"]), "index": np.arange(-8, 0, dtype=np.float32),
        "up": experts("L0_ffn_shared_up", "L0_ffn_routed_up", 2),
        "down": experts("L0_ffn_shared_down", "L0_ffn_routed_down", 8),
        "aq": k_tiles(i[c + "attn_Wq"].T), "ak": k_tiles(i[c + "attn_Wk"].T), "av": k_tiles(i[c + "attn_Wv"].T),
        "ao": k_tiles(i[c + "attn_Wo"].T), "lq": block_diagonal(i[c + "attn_Wq_lsr"]),
        "lk": block_diagonal(i[c + "attn_Wk_lsr"]), "tri": tri, "arows": rows(c + "attn_bv", c + "attn_bo"),
        "acols": np.ascontiguousarray(rows(c + "attn_bq", c + "attn_bk").reshape(2, KD, P).transpose(2, 0, 1)),
        "rq": by_heads(i[c + "xattn_W_Q"]), "rk": by_heads(i[c + "xattn_W_K"]), "rv": by_heads(i[c + "xattn_W_V"]),
        "rg": k_tiles(i[c + "xattn_g_w"].T), "ro": k_tiles(i[c + "xattn_out_w"].T),
        "rrows": rows(c + "xattn_g_b", c + "xattn_out_b"), "table": retention_tables(),
        "own": (index[:, None] // 32 == np.arange(64)[None] // 16).astype(np.float32),
        "keep": (index[:, None] <= index[None]).astype(np.float32),
        "s1": k_tiles(i[c + "ffn_sw1"]), "s3": k_tiles(i[c + "ffn_sw3"]), "s2": k_tiles(i[c + "ffn_sw2"]),
        "w1": np.ascontiguousarray(i[c + "ffn_w1"].reshape(8, 2, P, D).transpose(2, 0, 1, 3)),
        "w2": np.ascontiguousarray(i[c + "ffn_w2"].reshape(8, 2, P, D).transpose(2, 0, 1, 3)),
        "hcols": np.ascontiguousarray(np.concatenate(
            [i[c + n].reshape(-1, P).T for n in ("ffn_sb1", "ffn_sb3", "ffn_b1")], 1)),
        "hrows": np.concatenate([i[c + "ffn_sb2"][None], i[c + "ffn_b2"]])[None],
        "ident": np.eye(P, dtype=np.float32),
    }


def kernel(**inputs):
    import concourse.bacc as bacc
    from concourse.bass_utils import run_bass_kernel_spmd

    nc = bacc.Bacc("TRN2", target_bir_lowering=False, num_devices=1)
    arrays, aps = {}, {}
    for name, a in laid_out({k: np.asarray(v) for k, v in inputs.items()}).items():
        arrays[f"in_{name}"] = np.ascontiguousarray(a)
        aps[name] = nc.dram_tensor(f"in_{name}", a.shape, mybir.dt.from_np(a.dtype), kind="ExternalInput").ap()
    out = nc.dram_tensor("out_x", (TOK, D), F32, kind="ExternalOutput").ap()
    decoder_kernel(nc, aps, out)
    result = run_bass_kernel_spmd(nc, [arrays], core_ids=[0])
    return result.results[0]["out_x"].reshape(NB, L, D)
```
